# Optimizing a Trainium2 kernel written in Bass

```python
import numpy as np
import jax
import jax.numpy as jnp

def _softmax(x, axis=-1):
    return jax.nn.softmax(x, axis=axis)

def _gelu(x):
    return jax.nn.gelu(x, approximate=True)

def _silu(x):
    return jax.nn.silu(x)

def _sigmoid(x):
    return jax.nn.sigmoid(x)

def _layernorm(x, axis=-1, eps=1e-05):
    m = jnp.mean(x, axis=axis, keepdims=True)
    v = jnp.var(x, axis=axis, keepdims=True)
    return (x - m) / jnp.sqrt(v + eps)

def _scatter_add(tgt, idx, src, axis=0):
    return tgt.at[idx].add(src)

def _segment_sum(src, seg, n):
    return jax.ops.segment_sum(src, seg, n)
kernel_name = 'mk_decoder_preln_d1_seqx_r8_47845d'

def setup_inputs(seed: int=0):
    np.random.seed(seed)
    _w = jnp.asarray

    def _rec_inputs():
        import jax
        import jax.numpy as jnp
        _rk = jax.random.key(seed)
        x = -7.109e-05 + 0.9999 * jax.random.normal(jax.random.fold_in(_rk, 1), (4, 256, 256), jnp.float32)
        _lenS = 256 - jax.random.randint(jax.random.fold_in(_rk, 7), (4,), 0, max(1, 256 // 4) + 1, jnp.int32)
        _lenS2 = 256 - jax.random.randint(jax.random.fold_in(_rk, 8), (4,), 0, max(1, 256 // 4) + 1, jnp.int32)
        _ctx_512P = jax.random.normal(jax.random.fold_in(_rk, 11), (4, 16, 64), jnp.float32)
        _ctx_512c = jax.random.dirichlet(jax.random.fold_in(_rk, 511), 0.3 * jnp.ones((16,), jnp.float32), (4, 256))
        _ctx_512t = jnp.einsum('bsk,bkd->bsd', _ctx_512c, _ctx_512P)
        _ctx_512t = _ctx_512t * jax.lax.rsqrt(jnp.mean(jnp.square(_ctx_512t)) + 1e-12) * 0.953939
        ctx_512 = 2.81802e-05 + 1.00001 * (_ctx_512t + 0.3 * jax.random.normal(jax.random.fold_in(_rk, 611), (4, 256, 64), jnp.float32))
        return (x, ctx_512)
    x, ctx_512 = _rec_inputs()

    def _L0_attn_setup():
        import math
        import jax, jax.numpy as jnp
        import numpy as np
        EMBED_DIM = 256
        NUM_HEADS = 16
        HEAD_DIM = EMBED_DIM // NUM_HEADS
        CHUNK = 128
        RMS_EPS = 1e-05

        def _build_slopes(n):

            def pow2(n):
                start = 2.0 ** (-2.0 ** (-(math.log2(n) - 3)))
                return [start * start ** i for i in range(n)]
            if math.log2(n).is_integer():
                s = pow2(n)
            else:
                closest = 2 ** math.floor(math.log2(n))
                s = pow2(closest) + pow2(2 * closest)[0::2][:n - closest]
            return jnp.asarray(s, dtype=jnp.float32)

        def _rotary(x_BTHD, offset=0):
            T, D = (x_BTHD.shape[1], x_BTHD.shape[-1])
            freq = (1.0 / 1024.0) ** jnp.linspace(0.0, 1.0, D // 4, dtype=jnp.float32)
            freq = jnp.concatenate([freq, jnp.zeros(D // 4, dtype=jnp.float32)])
            t = jnp.arange(offset, offset + T, dtype=jnp.float32)
            theta = t[:, None] * freq[None, :]
            cos = jnp.cos(theta)[None, :, None, :]
            sin = jnp.sin(theta)[None, :, None, :]
            x1, x2 = jnp.split(x_BTHD.astype(jnp.float32), 2, axis=-1)
            y1 = x1 * cos + x2 * sin
            y2 = -x1 * sin + x2 * cos
            return jnp.concatenate([y1, y2], axis=-1).astype(x_BTHD.dtype)

        def _lightning_attn(q, k, v, slopes):
            B, H, T, D = q.shape
            C = CHUNK
            NC = T // C
            r = jnp.exp(-slopes)
            i = jnp.arange(C, dtype=jnp.float32)
            q_decay = r[:, None] ** (i[None, :] + 1.0)
            k_decay = r[:, None] ** (C - 1.0 - i[None, :])
            diff = i[:, None] - i[None, :]
            mask = diff >= 0
            dmask = jnp.where(mask[None], r[:, None, None] ** jnp.where(mask, diff, 0.0)[None], 0.0)
            r_C = r ** float(C)

            def reshape_chunks(x):
                return x.reshape(B, H, NC, C, D).transpose(2, 0, 1, 3, 4)
            qc, kc, vc = (reshape_chunks(q), reshape_chunks(k), reshape_chunks(v))

            def step(kv, qkv):
                qi, ki, vi = qkv
                inter = jnp.einsum('bhcd,bhde->bhce', qi * q_decay[None, :, :, None], kv)
                scores = jnp.einsum('bhcd,bhsd->bhcs', qi, ki) * dmask[None]
                intra = jnp.einsum('bhcs,bhse->bhce', scores, vi)
                kv_new = r_C[None, :, None, None] * kv + jnp.einsum('bhcd,bhce->bhde', ki * k_decay[None, :, :, None], vi)
                return (kv_new, inter + intra)
            kv0 = jnp.zeros((B, H, D, D), dtype=q.dtype)
            _, out = jax.lax.scan(step, kv0, (qc, kc, vc))
            return out.transpose(1, 2, 0, 3, 4).reshape(B, H, T, D)

        def _rms_norm(x, w):
            var = jnp.mean(jnp.square(x), axis=-1, keepdims=True)
            return x * jax.lax.rsqrt(var + RMS_EPS) * w
        key = jax.random.key(seed)
        ks = jax.random.split(key, 6)
        sc = 1.0 / math.sqrt(EMBED_DIM)
        return {'x': jax.random.normal(ks[0], (4, 512, EMBED_DIM), dtype=jnp.float32), 'Wq': jax.random.normal(ks[1], (EMBED_DIM, EMBED_DIM), dtype=jnp.float32) * sc, 'Wk': jax.random.normal(ks[2], (EMBED_DIM, EMBED_DIM), dtype=jnp.float32) * sc, 'Wv': jax.random.normal(ks[3], (EMBED_DIM, EMBED_DIM), dtype=jnp.float32) * sc, 'Wo': jax.random.normal(ks[4], (EMBED_DIM, EMBED_DIM), dtype=jnp.float32) * sc, 'rms_w': jnp.ones((EMBED_DIM,), dtype=jnp.float32)}
    _L0_attn_all = _L0_attn_setup()
    _L0_attn_in = {k: v for k, v in _L0_attn_all.items() if k in ('Wq', 'Wk', 'Wv', 'Wo', 'rms_w')}
    del _L0_attn_all

    def _L0_xattn_setup():
        import jax, jax.numpy as jnp
        import numpy as np
        EPS = 1e-06
        IMAGE_DIMS = 256
        key = jax.random.key(seed)
        k1, k2, k3 = jax.random.split(key, 3)
        B, I, J, D = (16, 256, 256, 64)
        p = jax.random.normal(k1, (B, I, J), dtype=jnp.float32)
        k_v = jax.random.normal(k2, (B, J, D), dtype=jnp.float32)
        W_k = jax.random.normal(k3, (D, D), dtype=jnp.float32) * (1.0 / np.sqrt(D))
        b_k = jnp.zeros((D,), dtype=jnp.float32)
        ln_gamma = jnp.ones((J,), dtype=jnp.float32)
        ln_beta = jnp.zeros((J,), dtype=jnp.float32)
        return {'p': p, 'k_v': k_v, 'W_k': W_k, 'b_k': b_k, 'ln_gamma': ln_gamma, 'ln_beta': ln_beta}
    _L0_xattn_all = _L0_xattn_setup()
    _L0_xattn_in = {k: v for k, v in _L0_xattn_all.items() if k in ('W_k', 'b_k', 'ln_gamma', 'ln_beta')}
    del _L0_xattn_all

    def _L0_ffn_setup():
        import jax, jax.numpy as jnp
        import numpy as np
        K_TOP = 2
        key = jax.random.key(seed)
        k0, k1, k2 = jax.random.split(key, 3)
        B, S, D, E, F = (4, 256, 256, 8, 256)
        x = jax.random.normal(k0, (B, S, D), dtype=jnp.float32)
        Wr = jax.random.normal(k1, (D, E), dtype=jnp.float32) * 0.02
        We = jax.random.normal(k2, (E, D, F), dtype=jnp.float32) * 0.02
        be = jnp.zeros((E, F), dtype=jnp.float32)
        return {'x': x, 'Wr': Wr, 'We': We, 'be': be}
    _L0_ffn_all = _L0_ffn_setup()
    _L0_ffn_in = {k: v for k, v in _L0_ffn_all.items() if k in ('Wr', 'We', 'be')}
    del _L0_ffn_all
    return {'x': x, 'ctx_512': ctx_512, 'L0_attn_Wq': _L0_attn_in['Wq'], 'L0_attn_Wk': _L0_attn_in['Wk'], 'L0_attn_Wv': _L0_attn_in['Wv'], 'L0_attn_Wo': _L0_attn_in['Wo'], 'L0_attn_rms_w': _L0_attn_in['rms_w'], 'L0_xattn_W_k': _L0_xattn_in['W_k'], 'L0_xattn_b_k': _L0_xattn_in['b_k'], 'L0_xattn_ln_gamma': _L0_xattn_in['ln_gamma'], 'L0_xattn_ln_beta': _L0_xattn_in['ln_beta'], 'L0_ffn_Wr': _L0_ffn_in['Wr'], 'L0_ffn_We': _L0_ffn_in['We'], 'L0_ffn_be': _L0_ffn_in['be']}

def reference(x, ctx_512, L0_attn_Wq, L0_attn_Wk, L0_attn_Wv, L0_attn_Wo, L0_attn_rms_w, L0_xattn_W_k, L0_xattn_b_k, L0_xattn_ln_gamma, L0_xattn_ln_beta, L0_ffn_Wr, L0_ffn_We, L0_ffn_be):
    import jax
    import jax.numpy as jnp

    def _L0_attn_ref(x, Wq, Wk, Wv, Wo, rms_w):
        import math
        import jax, jax.numpy as jnp
        import numpy as np
        EMBED_DIM = 256
        NUM_HEADS = 16
        HEAD_DIM = EMBED_DIM // NUM_HEADS
        CHUNK = 128
        RMS_EPS = 1e-05

        def _build_slopes(n):

            def pow2(n):
                start = 2.0 ** (-2.0 ** (-(math.log2(n) - 3)))
                return [start * start ** i for i in range(n)]
            if math.log2(n).is_integer():
                s = pow2(n)
            else:
                closest = 2 ** math.floor(math.log2(n))
                s = pow2(closest) + pow2(2 * closest)[0::2][:n - closest]
            return jnp.asarray(s, dtype=jnp.float32)

        def _rotary(x_BTHD, offset=0):
            T, D = (x_BTHD.shape[1], x_BTHD.shape[-1])
            freq = (1.0 / 1024.0) ** jnp.linspace(0.0, 1.0, D // 4, dtype=jnp.float32)
            freq = jnp.concatenate([freq, jnp.zeros(D // 4, dtype=jnp.float32)])
            t = jnp.arange(offset, offset + T, dtype=jnp.float32)
            theta = t[:, None] * freq[None, :]
            cos = jnp.cos(theta)[None, :, None, :]
            sin = jnp.sin(theta)[None, :, None, :]
            x1, x2 = jnp.split(x_BTHD.astype(jnp.float32), 2, axis=-1)
            y1 = x1 * cos + x2 * sin
            y2 = -x1 * sin + x2 * cos
            return jnp.concatenate([y1, y2], axis=-1).astype(x_BTHD.dtype)

        def _lightning_attn(q, k, v, slopes):
            B, H, T, D = q.shape
            C = CHUNK
            NC = T // C
            r = jnp.exp(-slopes)
            i = jnp.arange(C, dtype=jnp.float32)
            q_decay = r[:, None] ** (i[None, :] + 1.0)
            k_decay = r[:, None] ** (C - 1.0 - i[None, :])
            diff = i[:, None] - i[None, :]
            mask = diff >= 0
            dmask = jnp.where(mask[None], r[:, None, None] ** jnp.where(mask, diff, 0.0)[None], 0.0)
            r_C = r ** float(C)

            def reshape_chunks(x):
                return x.reshape(B, H, NC, C, D).transpose(2, 0, 1, 3, 4)
            qc, kc, vc = (reshape_chunks(q), reshape_chunks(k), reshape_chunks(v))

            def step(kv, qkv):
                qi, ki, vi = qkv
                inter = jnp.einsum('bhcd,bhde->bhce', qi * q_decay[None, :, :, None], kv)
                scores = jnp.einsum('bhcd,bhsd->bhcs', qi, ki) * dmask[None]
                intra = jnp.einsum('bhcs,bhse->bhce', scores, vi)
                kv_new = r_C[None, :, None, None] * kv + jnp.einsum('bhcd,bhce->bhde', ki * k_decay[None, :, :, None], vi)
                return (kv_new, inter + intra)
            kv0 = jnp.zeros((B, H, D, D), dtype=q.dtype)
            _, out = jax.lax.scan(step, kv0, (qc, kc, vc))
            return out.transpose(1, 2, 0, 3, 4).reshape(B, H, T, D)

        def _rms_norm(x, w):
            var = jnp.mean(jnp.square(x), axis=-1, keepdims=True)
            return x * jax.lax.rsqrt(var + RMS_EPS) * w
        B, T, E = x.shape
        H, D = (NUM_HEADS, HEAD_DIM)
        q = (x @ Wq).reshape(B, T, H, D)
        k = (x @ Wk).reshape(B, T, H, D)
        v = (x @ Wv).reshape(B, T, H, D)
        q = _rotary(q)
        k = _rotary(k)
        q, k, v = (t.transpose(0, 2, 1, 3) for t in (q, k, v))
        slopes = _build_slopes(H)
        attn = _lightning_attn(q, k, v, slopes)
        attn = attn.transpose(0, 2, 1, 3).reshape(B, T, E)
        attn = _rms_norm(attn, rms_w)
        return attn @ Wo

    def _L0_xattn_ref(p, k_v, W_k, b_k, ln_gamma, ln_beta):
        import jax, jax.numpy as jnp
        import numpy as np
        EPS = 1e-06
        IMAGE_DIMS = 256
        kv = k_v @ W_k.T + b_k
        out = jnp.einsum('bij,bjd->bid', p, kv)
        scale = IMAGE_DIMS ** (-0.5)
        sim = jnp.einsum('bid,bjd->bij', out, kv) * scale
        mu = jnp.mean(sim, axis=-1, keepdims=True)
        var = jnp.var(sim, axis=-1, keepdims=True)
        sim = (sim - mu) * jax.lax.rsqrt(var + EPS) * ln_gamma + ln_beta
        attn = jax.nn.softmax(sim, axis=-1)
        return attn

    def _L0_ffn_ref(x, Wr, We, be):
        import jax, jax.numpy as jnp
        import numpy as np
        K_TOP = 2
        logits = jnp.einsum('bsd,de->bse', x, Wr)
        w, sel = jax.lax.top_k(logits, K_TOP)
        w = jax.nn.softmax(w, axis=-1)
        E = We.shape[0]
        gate = jnp.einsum('bsk,bske->bse', w, jax.nn.one_hot(sel, E, dtype=w.dtype))
        out = jnp.zeros(x.shape[:2] + (We.shape[2],), dtype=x.dtype)
        for e in range(E):
            out = out + gate[..., e:e + 1] * (jnp.einsum('bsd,df->bsf', x, We[e]) + be[e])
        return out
    x = x + _L0_attn_ref(_layernorm(x, axis=-1), L0_attn_Wq, L0_attn_Wk, L0_attn_Wv, L0_attn_Wo, L0_attn_rms_w)
    x = x + _L0_xattn_ref(_layernorm(x, axis=-1), ctx_512, L0_xattn_W_k, L0_xattn_b_k, L0_xattn_ln_gamma, L0_xattn_ln_beta)
    x = x + _L0_ffn_ref(_layernorm(x, axis=-1), L0_ffn_Wr, L0_ffn_We, L0_ffn_be)
    return x

_drawn_inputs = setup_inputs


def setup_inputs(seed=0):
    import zlib

    import numpy as np

    out = dict(_drawn_inputs(seed))
    spreads = {'L0_attn_rms_w': (1.0, 0.2),
     'L0_xattn_b_k': (0.0, 0.8),
     'L0_xattn_ln_gamma': (1.0, 0.6),
     'L0_xattn_ln_beta': (0.0, 0.8),
     'L0_ffn_be': (0.0, 0.1)}
    factors = {'ctx_512': 5.503, 'L0_xattn_W_k': 8.0}
    for name, (base, spread) in spreads.items():
        noise = np.random.default_rng([zlib.crc32(name.encode()), seed]).standard_normal(out[name].shape)
        drawn = base * np.exp(spread * noise) if base else spread * noise
        out[name] = jnp.asarray(drawn.astype(out[name].dtype))
    for name, factor in factors.items():
        out[name] = (out[name] * factor).astype(out[name].dtype)
    return out
```

```python
from contextlib import ExitStack

import numpy as np

import concourse.bass as bass
from concourse import mybir

F32 = mybir.dt.float32
U32 = mybir.dt.uint32
ALU = mybir.AluOpType
ACT = mybir.ActivationFunctionType
AX_X = mybir.AxisListType.X

P = 128
B, T, D = 4, 256, 256
TILES = T // P
KC = D // P
H, DH = 16, 16
GROUPS = H * DH // P
PAIRS = 4
ROT = DH // 4
DC = 64
E, TOP = 8, 2
UNITS = TILES * E // 2
LN_EPS, RMS_EPS, SIM_EPS = 1e-5, 1e-5, 1e-6
SIM_SCALE = T ** -0.5

C_IDENT = 0
C_COS = C_IDENT + P
C_SIN = C_COS + TILES * ROT
C_KDEC = C_SIN + TILES * 2 * ROT
C_QDEC = C_KDEC + H
C_PAR = C_QDEC + GROUPS * P
C_BLOCK = C_PAR + 2
C_IOTA = C_BLOCK + P
C_ALL = C_IOTA + E


def shape_constants():
    f = np.float32
    start = 2.0 ** (-2.0 ** (-(np.log2(H) - 3)))
    slopes = np.array([start * start ** i for i in range(H)], f)
    r = np.exp(-slopes.astype(np.float64))
    pos = np.arange(P)
    c = np.zeros((P, C_ALL), f)
    c[:, C_IDENT:C_IDENT + P] = np.eye(P, dtype=f)
    freq = (f(1.0 / 1024.0) ** np.linspace(0.0, 1.0, ROT, dtype=f)).astype(f)
    theta = (np.arange(T, dtype=f)[:, None] * freq[None, :]).astype(f).astype(np.float64)
    cos = np.cos(theta).reshape(TILES, P, ROT).transpose(1, 0, 2)
    sin = np.sin(theta).reshape(TILES, P, ROT).transpose(1, 0, 2)
    c[:, C_COS:C_SIN] = cos.reshape(P, -1)
    c[:, C_SIN:C_KDEC] = np.stack([sin, -sin], axis=2).reshape(P, -1)
    c[:, C_KDEC:C_QDEC] = r[None, :] ** (P - 1.0 - pos[:, None])
    head_of_row = np.arange(P) // DH
    for g in range(GROUPS):
        c[:, C_QDEC + g * P:C_QDEC + (g + 1) * P] = r[g * 8 + head_of_row][:, None] ** (pos[None, :] + 1.0)
    c[:, C_PAR:C_BLOCK] = (head_of_row[:, None] % 2) == np.arange(2)[None, :]
    c[:, C_BLOCK:C_IOTA] = head_of_row[:, None] == head_of_row[None, :]
    c[:, C_IOTA:] = np.arange(E)[None, :]
    diff = pos[None, :] - pos[:, None]
    decay = np.zeros((P, PAIRS, GROUPS, 2, P), f)
    for j in range(PAIRS):
        for g in range(GROUPS):
            for par in range(2):
                rh = r[g * 8 + j * 2 + par]
                decay[:, j, g, par, :] = np.where(diff >= 0, rh ** np.maximum(diff, 0), 0.0)
    return c, decay.reshape(P, PAIRS * GROUPS * 2 * P)


class Count:

    def __init__(self, each):
        self.each, self.n, self.i = each, 0, 0

    def begin(self, i):
        self.i, self.n = i, 0

    def tick(self):
        self.n += 1
        return 1

    def now(self):
        return self.i * self.each + self.n


def decoder_layer(nc, x, ctx, wq, wk, wv, wo, rms_w, w_k, b_k, ln_gamma, ln_beta, wr, we, be,
                  consts, decay, out):
    with ExitStack() as stack:
        def sb(name, shape, dt=F32):
            return stack.enter_context(nc.sbuf_tensor(name, shape, dt))

        def sem(name):
            return stack.enter_context(nc.semaphore(name))

        cst = sb("cst", [P, C_ALL])
        dec = sb("dec", [P, PAIRS, 2 * GROUPS * P])
        w_qkv = sb("w_qkv", [P, KC, 3 * D])
        w_o = sb("w_o", [P, KC, D])
        rms_col = sb("rms_col", [P, KC])
        w_ctx = sb("w_ctx", [DC, DC])
        w_ctxT = sb("w_ctxT", [DC, DC])
        b_ctx = sb("b_ctx", [DC, 1])
        gam = sb("gam", [P, T])
        bet = sb("bet", [P, T])
        w_r = sb("w_r", [P, KC, E])
        w_e = sb("w_e", [P, KC, E, D])
        b_e = sb("b_e", [E, D])
        nhalf = sb("nhalf", [P, 2])
        onescol = sb("onescol", [P, 1])
        ident = cst[:, C_IDENT:C_IDENT + P]
        xin = sb("xin", [P, TILES, D])
        cin = sb("cin", [P, TILES, DC])
        ctxT = sb("ctxT", [DC, T])
        kvT = sb("kvT", [DC, T])
        kv = sb("kv", [P, TILES, DC])
        stats = sb("stats", [P, TILES, 6])
        mv = sb("mv", [P, TILES, 2])
        ve = sb("ve", [P, TILES])
        rs = sb("rs", [P, TILES])
        norm = sb("norm", [P, TILES, D])
        normT = sb("normT", [P, KC, T])
        qk = sb("qk", [P, TILES, 2 * D])
        rot_a = sb("rot_a", [P, TILES, 2 * H, 2, ROT])
        rot_b = sb("rot_b", [P, TILES, 2 * H, 2, ROT])
        vpad = sb("vpad", [P, TILES, H, 2 * DH])
        qx = sb("qx", [P, TILES, GROUPS, 2, P])
        kT = sb("kT", [P, TILES, GROUPS, P])
        kd = sb("kd", [P, D])
        qd = sb("qd", [P, GROUPS, P])
        state = sb("state", [P, GROUPS, P])
        probs = sb("probs", [P, TILES, PAIRS, 2 * GROUPS * P])
        attT = sb("attT", [P, TILES, GROUPS, P])
        sqT = sb("sqT", [P, TILES, GROUPS, P])
        rms_ve = sb("rms_ve", [P, TILES])
        rms_rs = sb("rms_rs", [P, TILES])
        x1 = sb("x1", [P, TILES, D])
        pkvT = sb("pkvT", [DC, T])
        sim_b = sb("sim_b", [P, TILES])
        z = sb("z", [P, TILES, T])
        zg = sb("zg", [P, TILES, T])
        zb = sb("zb", [P, TILES, T])
        zmax = sb("zmax", [P, TILES])
        nmax = sb("nmax", [P, TILES])
        ez = sb("ez", [P, TILES, T])
        esum = sb("esum", [P, TILES])
        rsum = sb("rsum", [P, TILES])
        x2 = sb("x2", [P, TILES, D])
        h3T = sb("h3T", [P, KC, T])
        lg = sb("lg", [P, TILES, E])
        top = sb("top", [P, TILES, 8])
        idx = sb("idx", [P, TILES, 8], U32)
        idxf = sb("idxf", [P, TILES, TOP])
        onehot = sb("onehot", [P, TOP, TILES, E])
        gdiff = sb("gdiff", [P, TILES])
        gexp = sb("gexp", [P, TILES])
        gden = sb("gden", [P, TILES])
        gw = sb("gw", [P, TOP, TILES])
        gpart = sb("gpart", [P, TOP, TILES, E])
        gate = sb("gate", [P, TILES, E])
        gateT = sb("gateT", [E, T])
        acc = sb("acc", [P, TILES, D])
        outb = sb("outb", [P, TILES, D])

        bank = [stack.enter_context(nc.psum_tensor(f"bank{n}", [P, 512], F32)) for n in range(6)]
        ebank = [stack.enter_context(nc.psum_tensor(f"ebank{n}", [P, 2, D], F32)) for n in range(2)]

        s_x, s_ctx = sem("x_loaded"), sem("ctx_loaded")
        s_cst, s_dec, s_wqkv, s_wo, s_wx, s_gb, s_wr, s_be = (
            sem(f"{n}_loaded") for n in ("consts", "decay", "wqkv", "wo", "wctx", "gamma_beta", "wr", "be"))
        s_we = [sem(f"we{k}_loaded") for k in range(KC)]
        s_const = sem("pool_consts_ready")
        v_step = sem("vector_step")
        s_wo_scaled = sem("wo_scaled")
        s_wctxT_ps, s_wctxT = sem("wctxT_in_psum"), sem("wctxT_ready")
        s_var = [sem(f"ln{n}_variance") for n in (1, 2, 3)]
        s_rstd = [sem(f"ln{n}_rstd") for n in (1, 2, 3)]
        s_norm = [sem(f"ln{n}_normalized") for n in (1, 2, 3)]
        s_nT_ps = [sem(f"ln{n}_transposed") for n in (1, 2, 3)]
        s_nT = [sem(f"ln{n}_T_on_sbuf") for n in (1, 2, 3)]
        s_qkv_ps, s_qk, s_v = sem("qkv_in_psum"), sem("qk_on_sbuf"), sem("v_on_sbuf")
        s_rb, s_rot, s_kd = sem("rotary_cross_terms"), sem("rotated"), sem("k_decayed")
        s_qkT_ps, s_qkT, s_qd = sem("qkT_in_psum"), sem("qkT_on_sbuf"), sem("q_decayed")
        s_st_ps, s_st = sem("state_in_psum"), sem("state_masked")
        s_sc_ps, s_sc = sem("scores_in_psum"), sem("scores_decayed")
        s_at_ps, s_at = sem("attention_in_psum"), sem("attention_on_sbuf")
        s_ss, s_y = sem("square_sums"), sem("attention_projected")
        s_rms_var, s_rms_rstd, s_x1 = sem("rms_variance"), sem("rms_rstd"), sem("x1_ready")
        s_c_ps, s_c = sem("context_step_in_psum"), sem("context_step_on_sbuf")
        s_pk_ps, s_pk = sem("pkv_in_psum"), sem("pkv_on_sbuf")
        s_sim = sem("similarity_in_psum")
        s_sv, s_sr, s_sb = sem("sim_variance"), sem("sim_rstd"), sem("sim_shift")
        s_z, s_zg, s_nm, s_ez, s_x2 = (sem("sim_normalized"), sem("sim_scaled"), sem("sim_negmax"),
                                       sem("sim_exp"), sem("x2_ready"))
        s_lg, s_gd, s_ge, s_gate = sem("logits"), sem("gate_difference"), sem("gate_exp"), sem("gates_ready")
        s_gT_ps, s_gT, s_gb_ps, s_acc = (sem("gatesT_in_psum"), sem("gatesT_on_sbuf"),
                                         sem("expert_bias_in_psum"), sem("accumulator_ready"))
        s_ex, s_exd = sem("expert_pair_in_psum"), sem("expert_products_added")
        s_st0, s_st1 = sem("tile0_stored"), sem("tile1_stored")

        block = stack.enter_context(nc.Block())

        def passes(eng, body):
            body(0, True, False)
            with eng.Fori(1, B) as i:
                body(i, True, True)
            body(B, False, True)

        @block.sync
        def _(sp):
            def load_x(i):
                sp.dma_start(xin[:], x[i].rearrange("(t p) d -> p t d", p=P)).then_inc(s_x, 16)

            load_x(0)
            sp.dma_start(cst[:], consts).then_inc(s_cst, 16)
            for n, w in enumerate((wq, wk, wv)):
                sp.dma_start(w_qkv[:, :, n * D:(n + 1) * D], w.rearrange("(c p) n -> p c n", p=P)).then_inc(s_wqkv, 16)
            sp.dma_start(dec[:], decay.rearrange("p (j n) -> p j n", j=PAIRS)).then_inc(s_dec, 16)
            sp.dma_start(w_e[:, 0], we.rearrange("e (c p) f -> p c e f", p=P)[:, 0]).then_inc(s_we[0], 16)
            sp.dma_start(w_e[:, 1], we.rearrange("e (c p) f -> p c e f", p=P)[:, 1]).then_inc(s_we[1], 16)

            def body(i, attentions, experts):
                if experts:
                    if attentions:
                        sp.wait_ge(s_x1, 2 * i)
                        load_x(i)
                        sp.wait_ge(s_c_ps, 3 * (i - 1) + 1)
                        sp.dma_start(cin[:], ctx[i].rearrange("(t p) d -> p t d", p=P)).then_inc(s_ctx, 16)
                    for t, done in enumerate((s_st0, s_st1)):
                        sp.wait_ge(s_exd, E * (TILES * (i - 1) + t + 1))
                        sp.dma_start(out[i - 1].rearrange("(t p) d -> p t d", p=P)[:, t, :], outb[:, t, :]).then_inc(done, 16)

            passes(sp, body)
            sp.wait_ge(s_st0, 16 * B)
            sp.wait_ge(s_st1, 16 * B)

        @block.gpsimd
        def _(pool):
            nc.gpsimd.memset(nhalf[:], -0.5).then_inc(s_const, 1)
            nc.gpsimd.memset(onescol[:], 1.0).then_inc(s_const, 1)
            nc.gpsimd.memset(vpad[:], 0.0).then_inc(s_const, 1)
            pool.wait_ge(s_const, 3)

            def rsqrt(dst, src, i, ready, done, each=1):
                pool.wait_ge(ready, each * (i + 1))
                nc.gpsimd.tensor_tensor(dst[:], src[:], nhalf[:], ALU.pow).then_inc(done, 1)

            def body(i, attentions, experts):
                if not attentions:
                    return
                rsqrt(rs, ve, i, s_var[0], s_rstd[0])
                for t in range(TILES):
                    pool.wait_ge(s_qk, 2 * i + t + 1)
                    v = qk[:, t, :].rearrange("p (h a r) -> p h a r", a=2, r=DH // 2)
                    for a in range(2):
                        at = C_SIN + (t * 2 + a) * ROT
                        sin = cst[:, at:at + ROT].unsqueeze(1).to_broadcast([P, 2 * H, ROT])
                        nc.gpsimd.tensor_tensor(rot_b[:, t, :, a, :], v[:, :, 1 - a, 0:ROT], sin,
                                                ALU.mult).then_inc(s_rb, 1)
                    if t == 0:
                        pool.wait_ge(s_rot, 2 * i + 1)
                        kdec = cst[:, C_KDEC:C_KDEC + H].unsqueeze(2).to_broadcast([P, H, DH])
                        nc.gpsimd.tensor_tensor(kd[:].rearrange("p (h d) -> p h d", h=H),
                                                qk[:, 0, D:].rearrange("p (h d) -> p h d", h=H), kdec,
                                                ALU.mult).then_inc(s_kd, 1)
                rsqrt(rms_rs, rms_ve, i, s_rms_var, s_rms_rstd, TILES)
                rsqrt(rs, ve, i, s_var[1], s_rstd[1])
                rsqrt(rs, ve, i, s_sv, s_sr)
                rsqrt(rs, ve, i, s_var[2], s_rstd[2])

            passes(pool, body)

        @block.scalar
        def _(act):
            act.dma_start(cin[:], ctx[0].rearrange("(t p) d -> p t d", p=P)).then_inc(s_ctx, 16)
            act.dma_start(w_ctx[:], w_k).then_inc(s_wx, 16)
            act.dma_start(b_ctx[:], b_k.rearrange("(p a) -> p a", a=1)).then_inc(s_wx, 16)
            act.dma_start(w_o[:], wo.rearrange("(c p) n -> p c n", p=P)).then_inc(s_wo, 16)
            for c in range(KC):
                act.dma_start(rms_col[:, c:c + 1], rms_w[c * P:(c + 1) * P].rearrange("(p a) -> p a", a=1)).then_inc(s_wo, 16)
            act.dma_start(gam[:], ln_gamma.partition_broadcast(P)).then_inc(s_gb, 16)
            act.dma_start(bet[:], ln_beta.partition_broadcast(P)).then_inc(s_gb, 16)
            act.dma_start(w_r[:], wr.rearrange("(c p) e -> p c e", p=P)).then_inc(s_wr, 16)
            act.dma_start(b_e[:], be).then_inc(s_be, 16)
            act.wait_ge(s_wctxT_ps, 1)
            act.copy(w_ctxT[:], bank[5][0:DC, 0:DC]).then_inc(s_wctxT, 1)
            act.wait_ge(s_cst, 16)
            act.wait_ge(s_wx, 32)
            act.wait_ge(s_const, 3)

            def body(i, attentions, experts):
                if not attentions:
                    return

                def transposed(n, banks, dst):
                    for t in range(TILES):
                        act.wait_ge(s_nT_ps[n], TILES * i + t + 1)
                        act.copy(dst[:, :, t * P:(t + 1) * P],
                                 banks[t][:, 0:D].rearrange("p (c n) -> p c n", c=KC)).then_inc(s_nT[n], 1)

                transposed(0, bank[0:3:2], normT)
                act.wait_ge(s_c_ps, 3 * i + 1)
                act.copy(ctxT[:], bank[5][0:DC, 0:T]).then_inc(s_c, 1)
                act.wait_ge(s_c_ps, 3 * i + 2)
                act.activation(kvT[:], bank[5][0:DC, 0:T], ACT.Identity, bias=b_ctx[:]).then_inc(s_c, 1)
                for t in range(TILES):
                    act.wait_ge(s_qkv_ps, TILES * i + t + 1)
                    act.copy(qk[:, t, :], bank[1 + t][:]).then_inc(s_qk, 1)
                    vp = vpad[:, t].rearrange("p (k a) n -> p k (a n)", a=2)
                    for a in range(2):
                        o = nc.scalar.copy(vp[:, :, a * 48:a * 48 + DH],
                                           bank[3 + t][:, 0:D].rearrange("p (k a n) -> p k a n", a=2, n=DH)[:, :, a, :])
                    o.then_inc(s_v, 1)
                act.wait_ge(s_c_ps, 3 * i + 3)
                act.copy(kv[:], bank[5][:, 0:TILES * DC].rearrange("p (t d) -> p t d", t=TILES)).then_inc(s_c, 1)
                for t in range(TILES):
                    act.wait_ge(s_qkT_ps, TILES * i + t + 1)
                    for par in range(2):
                        act.activation(qx[:, t, :, par, :], bank[t][:, 0:D].rearrange("p (g n) -> p g n", g=GROUPS),
                                       ACT.Copy, scale=cst[:, C_PAR + par:C_PAR + par + 1])
                    act.copy(kT[:, t], bank[t][:, D:].rearrange("p (g n) -> p g n", g=GROUPS)).then_inc(s_qkT, 1)
                for t in range(TILES):
                    act.wait_ge(s_at_ps, TILES * i + t + 1)
                    src = bank[t][:, 0:D].rearrange("p (g n) -> p g n", g=GROUPS)
                    act.activation(sqT[:, t], src, ACT.Square)
                    act.copy(attT[:, t], src).then_inc(s_at, 1)
                transposed(1, bank[4:6], normT)
                for t in range(TILES):
                    act.wait_ge(s_pk_ps, TILES * i + t + 1)
                    act.activation(pkvT[:, t * P:(t + 1) * P], bank[2 + t][0:DC, 0:P], ACT.Copy,
                                   scale=SIM_SCALE).then_inc(s_pk, 1)
                for t in range(TILES):
                    act.wait_ge(s_sb, i + 1)
                    act.activation(z[:, t], bank[t][:, 0:T], ACT.Identity, bias=sim_b[:, t:t + 1],
                                   scale=rs[:, t:t + 1]).then_inc(s_z, 1)
                for t in range(TILES):
                    act.wait_ge(s_nm, TILES * i + t + 1)
                    act.activation(ez[:, t], zb[:, t], ACT.Exp, bias=nmax[:, t:t + 1],
                                   accum_out=esum[:, t:t + 1]).then_inc(s_ez, 1)
                if experts:
                    act.wait_ge(s_ex, UNITS * i)
                transposed(2, bank[2:4], h3T)
                act.wait_ge(s_gd, i + 1)
                act.activation(gexp[:], gdiff[:], ACT.Exp).then_inc(s_ge, 1)
                act.wait_ge(s_gT_ps, i + 1)
                act.copy(gateT[:], bank[4][0:E, 0:T]).then_inc(s_gT, 1)

            passes(act, body)

        @block.vector
        def _(dve):
            v = Count(33)

            def layernorm(n, src, i):
                for t in range(TILES):
                    nc.vector.bn_stats(stats[:, t, :], src[:, t, :]).then_inc(v_step, v.tick())
                dve.drain()
                for t in range(TILES):
                    nc.vector.bn_aggr(mv[:, t, :], stats[:, t, :]).then_inc(v_step, v.tick())
                dve.wait_ge(v_step, v.now())
                nc.vector.tensor_scalar(ve[:], mv[:, :, 1], LN_EPS, None, ALU.add).then_inc(s_var[n], 1)
                dve.wait_ge(s_rstd[n], i + 1)
                for t in range(TILES):
                    nc.vector.tensor_scalar(norm[:, t, :], src[:, t, :], mv[:, t, 0:1], rs[:, t:t + 1],
                                            ALU.subtract, ALU.mult).then_inc(s_norm[n], 1)

            def add_experts(i, u):
                t, q = divmod(u, E // 2)
                dve.wait_ge(s_ex, UNITS * i + u + 1)
                for k in range(2):
                    e = 2 * q + k
                    last = e == E - 1
                    if last:
                        dve.wait_ge(s_st0 if t == 0 else s_st1, 16 * i)
                    nc.vector.scalar_tensor_tensor(
                        out=outb[:, t, :] if last else acc[:, t, :], in0=ebank[q % 2][:, k, :],
                        scalar=gate[:, t, e:e + 1], in1=acc[:, t, :], op0=ALU.mult,
                        op1=ALU.add).then_inc(s_exd, 1)
                    if not last:
                        dve.wait_ge(s_exd, E * TILES * i + 2 * u + k + 1)

            dve.wait_ge(s_wo, 16 * (1 + KC))
            for c in range(KC):
                nc.vector.tensor_scalar(w_o[:, c, :], w_o[:, c, :], rms_col[:, c:c + 1], None,
                                        ALU.mult).then_inc(s_wo_scaled, 1)
            dve.wait_ge(s_cst, 16)
            dve.wait_ge(s_dec, 16)
            dve.wait_ge(s_gb, 32)

            def body(i, attentions, experts):
                v.begin(i)

                def expert_unit(u):
                    if experts:
                        add_experts(i - 1, u)

                if not attentions:
                    for u in range(UNITS):
                        expert_unit(u)
                    return
                dve.wait_ge(s_x, 16 * (i + 1))
                layernorm(0, xin, i)
                expert_unit(0)
                for t in range(TILES):
                    dve.wait_ge(s_qk, TILES * i + t + 1)
                    rows = qk[:, t, :].rearrange("p (h r) -> p h r", r=DH // 2)[:, :, 0:ROT]
                    cos = cst[:, C_COS + t * ROT:C_COS + (t + 1) * ROT].unsqueeze(1).to_broadcast([P, 4 * H, ROT])
                    ra = rot_a[:, t].rearrange("p h a r -> p (h a) r")
                    rb = rot_b[:, t].rearrange("p h a r -> p (h a) r")
                    nc.vector.tensor_tensor(ra, rows, cos, ALU.mult).then_inc(v_step, v.tick())
                    dve.wait_ge(v_step, v.now())
                    dve.wait_ge(s_rb, 4 * i + 2 * t + 2)
                    nc.vector.tensor_tensor(rows, ra, rb, ALU.add).then_inc(s_rot, 1)
                dve.wait_ge(s_qkT, TILES * i + 2)
                nc.vector.tensor_tensor(qd[:], bank[1][:, 0:D].rearrange("p (g n) -> p g n", g=GROUPS),
                                        cst[:, C_QDEC:C_QDEC + D].rearrange("p (g n) -> p g n", g=GROUPS),
                                        ALU.mult).then_inc(s_qd, 1)
                dve.wait_ge(s_st_ps, i + 1)
                nc.vector.tensor_tensor(state[:], bank[0][:, 0:D].rearrange("p (g n) -> p g n", g=GROUPS),
                                        cst[:, C_BLOCK:C_BLOCK + P].unsqueeze(1).to_broadcast([P, GROUPS, P]),
                                        ALU.mult).then_inc(s_st, 1)
                for t in range(TILES):
                    if t == 0:
                        expert_unit(1)
                    for j in range(PAIRS):
                        dve.wait_ge(s_sc_ps, PAIRS * (TILES * i + t) + j + 1)
                        nc.vector.tensor_tensor(probs[:, t, j, :], bank[2 + j][:], dec[:, j, :],
                                                ALU.mult).then_inc(s_sc, 1)
                    expert_unit(2 + t)
                dve.wait_ge(s_ss, TILES * i + 2)
                for t in range(TILES):
                    nc.vector.tensor_scalar(rms_ve[:, t:t + 1], bank[4 + t][:, 0:1], 1.0 / D, RMS_EPS,
                                            ALU.mult, ALU.add).then_inc(s_rms_var, 1)
                dve.wait_ge(s_rms_rstd, i + 1)
                for t in range(TILES):
                    dve.wait_ge(s_y, TILES * i + t + 1)
                    nc.vector.scalar_tensor_tensor(out=x1[:, t, :], in0=bank[2 + t][:, 0:D],
                                                   scalar=rms_rs[:, t:t + 1], in1=xin[:, t, :],
                                                   op0=ALU.mult, op1=ALU.add).then_inc(s_x1, 1)
                dve.wait_ge(s_x1, TILES * i + 2)
                layernorm(1, x1, i)
                expert_unit(4)
                expert_unit(5)
                for t in range(TILES):
                    dve.wait_ge(s_sim, TILES * i + t + 1)
                    nc.vector.bn_stats(stats[:, t, :], bank[t][:, 0:T]).then_inc(v_step, v.tick())
                dve.drain()
                for t in range(TILES):
                    nc.vector.bn_aggr(mv[:, t, :], stats[:, t, :]).then_inc(v_step, v.tick())
                dve.wait_ge(v_step, v.now())
                nc.vector.tensor_scalar(ve[:], mv[:, :, 1], SIM_EPS, None, ALU.add).then_inc(s_sv, 1)
                dve.wait_ge(s_sr, i + 1)
                nc.vector.scalar_tensor_tensor(out=sim_b[:], in0=mv[:, :, 0], scalar=-1.0, in1=rs[:],
                                               op0=ALU.mult, op1=ALU.mult).then_inc(s_sb, 1)
                for t in range(TILES):
                    dve.wait_ge(s_z, TILES * i + t + 1)
                    nc.vector.tensor_tensor(zg[:, t], z[:, t], gam[:], ALU.mult).then_inc(s_zg, 1)
                    dve.drain()
                    nc.vector.tensor_tensor_reduce(out=zb[:, t], in0=zg[:, t], in1=bet[:], scale=1.0,
                                                   scalar=-3.0e38, op0=ALU.add, op1=ALU.max,
                                                   accum_out=zmax[:, t:t + 1]).then_inc(v_step, v.tick())
                    dve.wait_ge(v_step, v.now())
                    nc.vector.tensor_scalar(nmax[:, t:t + 1], zmax[:, t:t + 1], -1.0, None,
                                            ALU.mult).then_inc(s_nm, 1)
                expert_unit(6)
                for t in range(TILES):
                    dve.wait_ge(s_ez, TILES * i + t + 1)
                    nc.vector.reciprocal(rsum[:, t:t + 1], esum[:, t:t + 1]).then_inc(v_step, v.tick())
                    dve.wait_ge(v_step, v.now())
                    nc.vector.scalar_tensor_tensor(out=x2[:, t, :], in0=ez[:, t], scalar=rsum[:, t:t + 1],
                                                   in1=x1[:, t, :], op0=ALU.mult, op1=ALU.add).then_inc(s_x2, 1)
                dve.wait_ge(s_x2, TILES * i + 2)
                layernorm(2, x2, i)
                expert_unit(7)
                dve.wait_ge(s_lg, i + 1)
                nc.vector.tensor_copy(lg[:], bank[4][:, 0:TILES * E].rearrange("p (t e) -> p t e", e=E)).then_inc(v_step, v.tick())
                dve.drain()
                for t in range(TILES):
                    nc.vector.max(top[:, t, :], lg[:, t, :]).then_inc(v_step, v.tick())
                dve.wait_ge(v_step, v.now())
                nc.vector.tensor_tensor(gdiff[:], top[:, :, 1], top[:, :, 0], ALU.subtract).then_inc(s_gd, 1)
                for t in range(TILES):
                    nc.vector.max_index(idx[:, t, :], top[:, t, :], lg[:, t, :]).then_inc(v_step, v.tick())
                dve.wait_ge(v_step, v.now())
                nc.vector.tensor_copy(idxf[:], idx[:, :, 0:TOP]).then_inc(v_step, v.tick())
                dve.wait_ge(v_step, v.now())
                iota = cst[:, C_IOTA:C_IOTA + E].unsqueeze(1).to_broadcast([P, TILES, E])
                for k in range(TOP):
                    nc.vector.tensor_tensor(onehot[:, k], iota, idxf[:, :, k:k + 1].to_broadcast([P, TILES, E]),
                                            ALU.is_equal)
                dve.wait_ge(s_ge, i + 1)
                nc.vector.tensor_scalar(gden[:], gexp[:], 1.0, None, ALU.add).then_inc(v_step, v.tick())
                dve.wait_ge(v_step, v.now())
                nc.vector.reciprocal(gw[:, 0, :], gden[:]).then_inc(v_step, v.tick())
                dve.wait_ge(v_step, v.now())
                nc.vector.tensor_tensor(gw[:, 1, :], gexp[:], gw[:, 0, :], ALU.mult).then_inc(v_step, v.tick())
                dve.wait_ge(v_step, v.now())
                for k in range(TOP):
                    nc.vector.tensor_tensor(gpart[:, k], onehot[:, k],
                                            gw[:, k, :].unsqueeze(2).to_broadcast([P, TILES, E]),
                                            ALU.mult).then_inc(v_step, v.tick())
                dve.wait_ge(v_step, v.now())
                nc.vector.tensor_tensor(gate[:], gpart[:, 0], gpart[:, 1], ALU.add).then_inc(s_gate, 1)
                dve.wait_ge(s_gb_ps, i + 1)
                nc.vector.tensor_tensor(acc[:], x2[:], bank[5][:].rearrange("p (t n) -> p t n", t=TILES),
                                        ALU.add).then_inc(s_acc, 1)
                dve.wait_ge(s_acc, i + 1)
                assert v.n == v.each, v.n

            passes(dve, body)

        @block.tensor
        def _(pe):
            pe.wait_ge(s_cst, 16)
            pe.wait_ge(s_wx, 32)
            pe.transpose(bank[5][0:DC, 0:DC], w_ctx[:], ident[0:DC, 0:DC]).then_inc(s_wctxT_ps, 1)
            pe.wait_ge(s_wctxT, 1)

            def expert(i, u):
                t, q = divmod(u, E // 2)
                if u >= 2:
                    pe.wait_ge(s_exd, 2 * (UNITS * i + u - 1))
                for c in range(KC):
                    mm = pe.matmul(ebank[q % 2][:], h3T[:, c, t * P:(t + 1) * P], w_e[:, c, 2 * q:2 * q + 2, :],
                                   start=(c == 0), stop=(c == KC - 1))
                mm.then_inc(s_ex, 1)

            def transposes(n, banks, i):
                for t in range(TILES):
                    pe.wait_ge(s_norm[n], TILES * i + t + 1)
                    for c in range(KC):
                        mm = pe.transpose(banks[t][:, c * P:(c + 1) * P], norm[:, t, c * P:(c + 1) * P], ident)
                    mm.then_inc(s_nT_ps[n], 1)

            def body(i, attentions, experts):
                first = isinstance(i, int) and i == 0

                def expert_unit(u):
                    if experts:
                        expert(i - 1, u)

                if experts:
                    pass
                if not attentions:
                    for u in range(UNITS):
                        expert_unit(u)
                    return
                pe.wait_ge(s_ctx, 16 * (i + 1))
                if not first:
                    pe.wait_ge(s_acc, i)
                transposes(0, bank[0:3:2], i)
                for t in range(TILES):
                    mm = pe.transpose(bank[5][0:DC, t * P:(t + 1) * P], cin[:, t, :], ident)
                mm.then_inc(s_c_ps, 1)
                expert_unit(0)
                if first:
                    pe.wait_ge(s_wqkv, 48)
                for t in range(TILES):
                    pe.wait_ge(s_nT[0], TILES * i + t + 1)
                    for c in range(KC):
                        pe.matmul(bank[1 + t][:], normT[:, c, t * P:(t + 1) * P], w_qkv[:, c, 0:2 * D],
                                  start=(c == 0), stop=(c == KC - 1))
                    pe.wait_ge(s_c, 3 * i + 1 + t)
                    for c in range(KC):
                        mm = pe.matmul(bank[3 + t][:, 0:D], normT[:, c, t * P:(t + 1) * P], w_qkv[:, c, 2 * D:],
                                       start=(c == 0), stop=(c == KC - 1))
                    mm.then_inc(s_qkv_ps, 1)
                    if t == 0:
                        pe.matmul(bank[5][0:DC, 0:T], w_ctxT[:], ctxT[:], start=True, stop=True).then_inc(s_c_ps, 1)
                for t in range(TILES):
                    mm = pe.transpose(bank[5][:, t * DC:(t + 1) * DC], kvT[:, t * P:(t + 1) * P], ident[0:DC, 0:DC])
                mm.then_inc(s_c_ps, 1)
                for t in range(TILES):
                    pe.wait_ge(s_rot, TILES * i + t + 1)
                    for b in range(2 * GROUPS):
                        mm = pe.transpose(bank[t][:, b * P:(b + 1) * P], qk[:, t, b * P:(b + 1) * P], ident)
                    mm.then_inc(s_qkT_ps, 1)
                    if t == 0:
                        expert_unit(1)
                pe.wait_ge(s_qkT, TILES * i + 1)
                pe.wait_ge(s_kd, i + 1)
                for g in range(GROUPS):
                    vg = vpad[:, 0].rearrange("p (k a) n -> p k (a n)", a=2)[:, g * PAIRS:(g + 1) * PAIRS]
                    vg = vg.rearrange("p k (u n) -> p k u n", n=DH)[:, :, 0:4:3, :]
                    mm = pe.matmul(bank[0][:, g * P:(g + 1) * P], kd[:, g * P:(g + 1) * P], vg,
                                   start=True, stop=True)
                mm.then_inc(s_st_ps, 1)

                def scores(t):
                    pe.wait_ge(s_qkT, TILES * i + t + 1)
                    for g in range(GROUPS):
                        for j in range(PAIRS):
                            if g == 0 and t > 0:
                                pe.wait_ge(s_sc, PAIRS * (TILES * i + t - 1) + j + 1)
                            mm = pe.matmul(bank[2 + j][:, g * D:(g + 1) * D], kT[32 * j:32 * j + 32, t, g, :],
                                           qx[32 * j:32 * j + 32, t, g, :, :], start=True, stop=True)
                            if g == GROUPS - 1:
                                mm.then_inc(s_sc_ps, 1)

                def attend(t):
                    if t == 0:
                        pe.wait_ge(s_st, i + 1)
                    else:
                        pe.wait_ge(s_qd, i + 1)
                    for g in range(GROUPS):
                        for par in range(2):
                            for j in range(PAIRS):
                                if g == 0 and par == 0:
                                    pe.wait_ge(s_sc, PAIRS * (TILES * i + t) + j + 1)
                                h = g * 8 + j * 2 + par
                                mm = pe.matmul(bank[t][32 * j:32 * j + 32, g * P:(g + 1) * P], vpad[:, t, h, :],
                                               probs[:, t, j, (2 * g + par) * P:(2 * g + par + 1) * P],
                                               start=(par == 0), stop=(par == 1 and t == 0))
                        if t == 1:
                            for j in range(PAIRS):
                                mm = pe.matmul(bank[t][32 * j:32 * j + 32, g * P:(g + 1) * P],
                                               state[:, g, 32 * j:32 * j + 32], qd[:, g, :], start=False, stop=True)
                    mm.then_inc(s_at_ps, 1)

                scores(0)
                expert_unit(2)
                scores(1)
                attend(0)
                expert_unit(3)
                attend(1)
                pe.wait_ge(s_sc, PAIRS * TILES * (i + 1))
                pe.wait_ge(s_wo_scaled, KC)
                for t in range(TILES):
                    pe.wait_ge(s_at, TILES * i + t + 1)
                    for g in range(GROUPS):
                        mm = pe.matmul(bank[4 + t][:, 0:1], sqT[:, t, g, :], onescol[:],
                                       start=(g == 0), stop=(g == GROUPS - 1))
                    mm.then_inc(s_ss, 1)
                    for g in range(GROUPS):
                        mm = pe.matmul(bank[2 + t][:, 0:D], attT[:, t, g, :], w_o[:, g, :],
                                       start=(g == 0), stop=(g == GROUPS - 1))
                    mm.then_inc(s_y, 1)
                expert_unit(4)
                transposes(1, bank[4:6], i)
                pe.wait_ge(s_c, 3 * i + 3)
                for t in range(TILES):
                    pe.wait_ge(s_nT[1], TILES * i + t + 1)
                    for c in range(TILES):
                        mm = pe.matmul(bank[2 + t][0:DC, 0:P], kv[:, c, :], normT[:, c, t * P:(t + 1) * P],
                                       start=(c == 0), stop=(c == TILES - 1))
                    mm.then_inc(s_pk_ps, 1)
                for t in range(TILES):
                    pe.wait_ge(s_pk, TILES * i + t + 1)
                    pe.matmul(bank[t][:, 0:T], pkvT[:, t * P:(t + 1) * P], kvT[:], start=True, stop=True).then_inc(s_sim, 1)
                expert_unit(5)
                expert_unit(6)
                expert_unit(7)
                transposes(2, bank[2:4], i)
                if first:
                    pe.wait_ge(s_wr, 16)
                for t in range(TILES):
                    pe.wait_ge(s_nT[2], TILES * i + t + 1)
                    for c in range(KC):
                        mm = pe.matmul(bank[4][:, t * E:(t + 1) * E], h3T[:, c, t * P:(t + 1) * P], w_r[:, c, :],
                                       start=(c == 0), stop=(c == KC - 1))
                mm.then_inc(s_lg, 1)
                if first:
                    pe.wait_ge(s_be, 16)
                    pe.wait_ge(s_we[0], 16)
                    pe.wait_ge(s_we[1], 16)
                pe.wait_ge(s_gate, i + 1)
                for t in range(TILES):
                    mm = pe.transpose(bank[4][0:E, t * P:(t + 1) * P], gate[:, t, :], ident)
                mm.then_inc(s_gT_ps, 1)
                pe.wait_ge(s_gT, i + 1)
                for t in range(TILES):
                    mm = pe.matmul(bank[5][:, t * D:(t + 1) * D], gateT[:, t * P:(t + 1) * P], b_e[:],
                                   start=True, stop=True)
                mm.then_inc(s_gb_ps, 1)

            passes(pe, body)


_INS = ["x", "ctx_512", "L0_attn_Wq", "L0_attn_Wk", "L0_attn_Wv", "L0_attn_Wo", "L0_attn_rms_w",
        "L0_xattn_W_k", "L0_xattn_b_k", "L0_xattn_ln_gamma", "L0_xattn_ln_beta",
        "L0_ffn_Wr", "L0_ffn_We", "L0_ffn_be"]


def kernel(**inputs):
    import concourse.bacc as _bacc
    from concourse.bass_utils import run_bass_kernel_spmd as _run

    nc = _bacc.Bacc("TRN2", target_bir_lowering=False, num_devices=1)
    arrays, args = {}, []
    small, decay = shape_constants()
    named = [(name, inputs[name]) for name in _INS] + [("consts", small), ("decay", decay)]
    for name, value in named:
        a = np.ascontiguousarray(value)
        arrays[f"in_{name}"] = a
        args.append(nc.dram_tensor(f"in_{name}", a.shape, mybir.dt.from_np(a.dtype), kind="ExternalInput").ap())
    args.append(nc.dram_tensor("out_0", (B, T, D), F32, kind="ExternalOutput").ap())
    decoder_layer(nc, *args)
    r = _run(nc, [arrays], core_ids=[0])
    return r.results[0]["out_0"]
```

```python
from contextlib import ExitStack

import numpy as np

import concourse.bass as bass
from concourse import mybir

F32 = mybir.dt.float32
F32R = mybir.dt.float32r
U32 = mybir.dt.uint32
ALU = mybir.AluOpType
ACT = mybir.ActivationFunctionType
AX_X = mybir.AxisListType.X

P = 128
B, T, D = 4, 256, 256
TILES = T // P
KC = D // P
H, DH = 16, 16
GROUPS = H * DH // P
PAIRS = 4
QUADS = H // 4
ROT = DH // 4
DC = 64
E, TOP = 8, 2
UNITS = TILES * E // 2
LN_EPS, RMS_EPS, SIM_EPS = 1e-5, 1e-5, 1e-6
SIM_SCALE = T ** -0.5
FRONT_STEPS, BACK_STEPS = 2, 14

C_IDENT = 0
C_COS = C_IDENT + P
C_SIN = C_COS + TILES * ROT
C_KDEC = C_SIN + TILES * 2 * ROT
C_QDEC = C_KDEC + H
C_PAR = C_QDEC + GROUPS * P
C_BLOCK = C_PAR + 4
C_IOTA = C_BLOCK + P
C_ALL = C_IOTA + E


def shape_constants():
    f = np.float32
    start = 2.0 ** (-2.0 ** (-(np.log2(H) - 3)))
    slopes = np.array([start * start ** i for i in range(H)], f)
    r = np.exp(-slopes.astype(np.float64))
    pos = np.arange(P)
    c = np.zeros((P, C_ALL), f)
    c[:, C_IDENT:C_IDENT + P] = np.eye(P, dtype=f)
    freq = (f(1.0 / 1024.0) ** np.linspace(0.0, 1.0, ROT, dtype=f)).astype(f)
    theta = (np.arange(T, dtype=f)[:, None] * freq[None, :]).astype(f).astype(np.float64)
    cos = np.cos(theta).reshape(TILES, P, ROT).transpose(1, 0, 2)
    sin = np.sin(theta).reshape(TILES, P, ROT).transpose(1, 0, 2)
    c[:, C_COS:C_SIN] = cos.reshape(P, -1)
    c[:, C_SIN:C_KDEC] = np.stack([sin, -sin], axis=2).reshape(P, -1)
    c[:, C_KDEC:C_QDEC] = r[None, :] ** (P - 1.0 - pos[:, None])
    head_of_row = np.arange(P) // DH
    for g in range(GROUPS):
        c[:, C_QDEC + g * P:C_QDEC + (g + 1) * P] = r[g * 8 + head_of_row][:, None] ** (pos[None, :] + 1.0)
    c[:, C_PAR:C_BLOCK] = (head_of_row[:, None] % 4) == np.arange(4)[None, :]
    c[:, C_BLOCK:C_IOTA] = head_of_row[:, None] == head_of_row[None, :]
    c[:, C_IOTA:] = np.arange(E)[None, :]
    diff = pos[None, :] - pos[:, None]
    decay = np.where(diff[:, None, :] >= 0, r[None, :, None] ** np.maximum(diff, 0)[:, None, :], 0.0)
    return c, decay.astype(f).reshape(P, H * P)


class Count:

    def __init__(self, each):
        self.each, self.n, self.i = each, 0, 0

    def begin(self, i):
        self.i, self.n = i, 0

    def tick(self):
        self.n += 1
        return 1

    def now(self):
        return self.i * self.each + self.n


def decoder_layer(nc, x, ctx, wq, wk, wv, wo, rms_w, w_k, b_k, ln_gamma, ln_beta, wr, we, be,
                  consts, decay, out):
    with ExitStack() as stack:
        def sb(name, shape, dt=F32):
            return stack.enter_context(nc.sbuf_tensor(name, shape, dt))

        def sem(name):
            return stack.enter_context(nc.semaphore(name))

        cst = sb("cst", [P, C_ALL])
        dec = sb("dec", [P, H, P])
        w_qkv = sb("w_qkv", [P, KC, 3 * D])
        w_qkv_s = [sb(f"w_qkv_{n}", [P, KC, 3 * D], F32R) for n in ("hi", "lo")]
        w_o = sb("w_o", [P, KC, D])
        rms_col = sb("rms_col", [P, KC])
        w_ctx = sb("w_ctx", [DC, DC])
        w_ctxT = sb("w_ctxT", [DC, DC])
        b_ctx = sb("b_ctx", [DC, 1])
        gam = sb("gam", [P, T])
        bet = sb("bet", [P, T])
        w_r = sb("w_r", [P, KC, E])
        w_r_s = [sb(f"w_r_{n}", [P, KC, E], F32R) for n in ("hi", "lo")]
        w_e = sb("w_e", [P, KC, E * D])
        w_e_s = [sb(f"w_e_{n}", [P, KC, E * D], F32R) for n in ("hi", "lo")]
        b_e = sb("b_e", [E, D])
        nhalf = sb("nhalf", [P, 2])
        onescol = sb("onescol", [P, 1])
        ident = cst[:, C_IDENT:C_IDENT + P]
        xin = sb("xin", [P, TILES, D])
        xres = sb("xres", [P, TILES, D])
        cin = sb("cin", [P, TILES, DC])
        ctxT = sb("ctxT", [DC, T])
        kvT = sb("kvT", [DC, T])
        kv = sb("kv", [P, TILES, DC])
        stats = [sb(f"stats{n}", [P, TILES, 6]) for n in range(4)]
        mv = [sb(f"mv{n}", [P, TILES, 2]) for n in range(4)]
        ve = [sb(f"ve{n}", [P, TILES]) for n in range(4)]
        rs = [sb(f"rs{n}", [P, TILES]) for n in range(4)]
        norm = [sb(f"norm{n}", [P, TILES, D]) for n in range(3)]
        h1T = [sb(f"h1T_{n}", [P, KC, T], F32R) for n in ("hi", "lo")]
        qk = sb("qk", [P, TILES, 2 * D])
        rot_a = sb("rot_a", [P, TILES, 2 * H, 2, ROT])
        rot_b = sb("rot_b", [P, TILES, 2 * H, 2, ROT])
        vpad = sb("vpad", [P, TILES, H, 2 * DH])
        qx = sb("qx", [P, TILES, GROUPS, 4, P])
        kT = sb("kT", [P, TILES, GROUPS, P])
        kd = sb("kd", [P, D])
        qd = sb("qd", [P, GROUPS, P])
        state = sb("state", [P, GROUPS, P])
        probs = sb("probs", [P, TILES, H, P])
        attT = sb("attT", [P, TILES, GROUPS, P])
        sqT = sb("sqT", [P, TILES, GROUPS, P])
        rms_ve = sb("rms_ve", [P, TILES])
        rms_rs = sb("rms_rs", [P, TILES])
        x1 = sb("x1", [P, TILES, D])
        pT = sb("pT", [P, KC, T])
        pkvT = sb("pkvT", [DC, T])
        sim_b = sb("sim_b", [P, TILES])
        z = sb("z", [P, TILES, T])
        zg = sb("zg", [P, TILES, T])
        zb = sb("zb", [P, TILES, T])
        zmax = sb("zmax", [P, TILES])
        nmax = sb("nmax", [P, TILES])
        ez = sb("ez", [P, TILES, T])
        esum = sb("esum", [P, TILES])
        rsum = sb("rsum", [P, TILES])
        x2 = sb("x2", [P, TILES, D])
        h3T = [sb(f"h3T_{n}", [P, KC, T], F32R) for n in ("hi", "lo")]
        lg = sb("lg", [P, TILES, E])
        top = sb("top", [P, TILES, 8])
        idx = sb("idx", [P, TILES, 8], U32)
        idxf = sb("idxf", [P, TILES, TOP])
        onehot = sb("onehot", [P, TOP, TILES, E])
        gdiff = sb("gdiff", [P, TILES])
        gexp = sb("gexp", [P, TILES])
        gden = sb("gden", [P, TILES])
        gw = sb("gw", [P, TOP, TILES])
        gpart = sb("gpart", [P, TOP, TILES, E])
        gate = sb("gate", [P, TILES, E])
        gateT = sb("gateT", [E, T])
        acc = sb("acc", [P, TILES, D])
        outb = sb("outb", [P, TILES, D])

        bank = [stack.enter_context(nc.psum_tensor(f"bank{n}", [P, 512], F32)) for n in range(6)]
        ebank = [stack.enter_context(nc.psum_tensor(f"ebank{n}", [P, 512], F32)) for n in range(2)]

        s_x, s_ctx = sem("x_loaded"), sem("ctx_loaded")
        s_cst, s_dec, s_wqkv, s_wo, s_wx, s_gb, s_wr, s_be = (
            sem(f"{n}_loaded") for n in ("consts", "decay", "wqkv", "wo", "wctx", "gamma_beta", "wr", "be"))
        s_we = [sem(f"we{k}_loaded") for k in range(KC)]
        s_const = sem("pool_consts_ready")
        s_hi, s_lo = sem("weights_high_parts"), sem("weights_low_parts")
        s_wqkv_hi, s_wqkv_lo = sem("wqkv_high_parts"), sem("wqkv_low_parts")
        v_front, v_back = sem("vector_front_step"), sem("vector_back_step")
        s_wo_scaled = sem("wo_scaled")
        s_wctxT_ps, s_wctxT = sem("wctxT_in_psum"), sem("wctxT_ready")
        s_var = [sem(f"ln{n}_variance") for n in (1, 2, 3)]
        s_rstd = [sem(f"ln{n}_rstd") for n in (1, 2, 3)]
        s_norm = [sem(f"ln{n}_normalized") for n in (1, 2, 3)]
        s_nT_ps = [sem(f"ln{n}_transposed") for n in (1, 2, 3)]
        s_nT = [sem(f"ln{n}_T_on_sbuf") for n in (1, 2, 3)]
        s_nT_lo = [sem(f"ln{n}_T_low_part") for n in (1, 2, 3)]
        s_xres = sem("residual_copied")
        s_qkv_ps, s_qk, s_v = sem("qkv_in_psum"), sem("qk_on_sbuf"), sem("v_on_sbuf")
        s_rb, s_rot, s_kd = sem("rotary_cross_terms"), sem("rotated"), sem("k_decayed")
        s_qkT_ps, s_qkT, s_qd = sem("qkT_in_psum"), sem("qkT_on_sbuf"), sem("q_decayed")
        s_st_ps, s_st = sem("state_in_psum"), sem("state_masked")
        s_sc_ps, s_sc = sem("scores_in_psum"), sem("scores_decayed")
        s_at_ps, s_at = sem("attention_in_psum"), sem("attention_on_sbuf")
        s_ss, s_y = sem("square_sums"), sem("attention_projected")
        s_rms_var, s_rms_rstd, s_x1 = sem("rms_variance"), sem("rms_rstd"), sem("x1_ready")
        s_c_ps, s_c = sem("context_step_in_psum"), sem("context_step_on_sbuf")
        s_pk_ps, s_pk = sem("pkv_in_psum"), sem("pkv_on_sbuf")
        s_sim = sem("similarity_in_psum")
        s_sv, s_sr, s_sb = sem("sim_variance"), sem("sim_rstd"), sem("sim_shift")
        s_z, s_nm, s_ez, s_x2 = (sem("sim_normalized"), sem("sim_negmax"), sem("sim_exp"), sem("x2_ready"))
        s_lg, s_gd, s_ge, s_gate = sem("logits"), sem("gate_difference"), sem("gate_exp"), sem("gates_ready")
        s_gT_ps, s_gT, s_gb_ps, s_acc = (sem("gatesT_in_psum"), sem("gatesT_on_sbuf"),
                                         sem("expert_bias_in_psum"), sem("accumulator_ready"))
        s_ex, s_exd = sem("expert_pair_in_psum"), sem("expert_products_added")
        s_st0, s_st1 = sem("tile0_stored"), sem("tile1_stored")

        block = stack.enter_context(nc.Block())

        def passes(eng, body):
            body(0, True, False, False)
            body(1, True, True, False)
            with eng.Fori(2, B) as i:
                body(i, True, True, True)
            body(B, False, True, True)
            body(B + 1, False, False, True)

        @block.sync
        def _(sp):
            def load_x(i):
                sp.dma_start(xin[:], x[i].rearrange("(t p) d -> p t d", p=P)).then_inc(s_x, 16)

            load_x(0)
            for n, w in enumerate((wq, wk, wv)):
                sp.dma_start(w_qkv[:, :, n * D:(n + 1) * D], w.rearrange("(c p) n -> p c n", p=P)).then_inc(s_wqkv, 16)
            sp.dma_start(dec[:], decay.rearrange("p (h n) -> p h n", h=H)).then_inc(s_dec, 16)
            for c in range(KC):
                sp.dma_start(w_e[:, c].rearrange("p (e f) -> p e f", e=E),
                             we.rearrange("e (c p) f -> p c e f", p=P)[:, c]).then_inc(s_we[c], 16)

            def body(i, front, back, rest):
                if front and back:
                    sp.wait_ge(s_norm[0], TILES * i)
                    sp.wait_ge(s_xres, i)
                    load_x(i)
                    sp.wait_ge(s_c_ps, 3 * (i - 1) + 1)
                    sp.dma_start(cin[:], ctx[i].rearrange("(t p) d -> p t d", p=P)).then_inc(s_ctx, 16)
                for t, done in ((0, s_st0), (1, s_st1)):
                    if rest:
                        b = i - 2
                        sp.wait_ge(s_exd, E * (TILES * b + t + 1))
                        sp.dma_start(out[b].rearrange("(t p) d -> p t d", p=P)[:, t, :], outb[:, t, :]).then_inc(done, 16)

            passes(sp, body)
            sp.wait_ge(s_st0, 16 * B)
            sp.wait_ge(s_st1, 16 * B)

        @block.gpsimd
        def _(pool):
            nc.gpsimd.memset(nhalf[:], -0.5).then_inc(s_const, 1)
            nc.gpsimd.memset(onescol[:], 1.0).then_inc(s_const, 1)
            nc.gpsimd.memset(vpad[:], 0.0).then_inc(s_const, 1)
            pool.wait_ge(s_const, 3)

            def rsqrt(dst, src, i, ready, done, each=1):
                pool.wait_ge(ready, each * (i + 1))
                nc.gpsimd.tensor_tensor(dst[:], src[:], nhalf[:], ALU.pow).then_inc(done, 1)

            def body(i, front, back, rest):
                if front:
                    rsqrt(rs[0], ve[0], i, s_var[0], s_rstd[0])
                if back:
                    rsqrt(rs[3], ve[3], i - 1, s_sv, s_sr)
                for t in range(TILES if front else 0):
                    pool.wait_ge(s_qk, TILES * i + t + 1)
                    v = qk[:, t, :].rearrange("p (h a r) -> p h a r", a=2, r=DH // 2)
                    for a in range(2):
                        at = C_SIN + (t * 2 + a) * ROT
                        sin = cst[:, at:at + ROT].unsqueeze(1).to_broadcast([P, 2 * H, ROT])
                        nc.gpsimd.tensor_tensor(rot_b[:, t, :, a, :], v[:, :, 1 - a, 0:ROT], sin,
                                                ALU.mult).then_inc(s_rb, 1)
                if front:
                    pool.wait_ge(s_rot, TILES * i + 1)
                    kdec = cst[:, C_KDEC:C_KDEC + H].unsqueeze(2).to_broadcast([P, H, DH])
                    nc.gpsimd.tensor_tensor(kd[:].rearrange("p (h d) -> p h d", h=H),
                                            qk[:, 0, D:].rearrange("p (h d) -> p h d", h=H), kdec,
                                            ALU.mult).then_inc(s_kd, 1)
                if back:
                    rsqrt(rs[2], ve[2], i - 1, s_var[2], s_rstd[2])
                if front and not back:
                    for c in range(KC):
                        pool.wait_ge(s_hi, 1 + c + 1)
                        nc.gpsimd.tensor_tensor(w_e_s[1][:, c], w_e[:, c], w_e_s[0][:, c].bitcast(F32),
                                                ALU.subtract).then_inc(s_lo, 1)
                if front:
                    rsqrt(rms_rs, rms_ve, i, s_rms_var, s_rms_rstd, TILES)
                    rsqrt(rs[1], ve[1], i, s_var[1], s_rstd[1])

            passes(pool, body)

        @block.scalar
        def _(act):
            act.dma_start(cst[:], consts).then_inc(s_cst, 16)
            act.dma_start(cin[:], ctx[0].rearrange("(t p) d -> p t d", p=P)).then_inc(s_ctx, 16)
            act.dma_start(w_ctx[:], w_k).then_inc(s_wx, 16)
            act.dma_start(b_ctx[:], b_k.rearrange("(p a) -> p a", a=1)).then_inc(s_wx, 16)
            act.dma_start(w_o[:], wo.rearrange("(c p) n -> p c n", p=P)).then_inc(s_wo, 16)
            for c in range(KC):
                act.dma_start(rms_col[:, c:c + 1], rms_w[c * P:(c + 1) * P].rearrange("(p a) -> p a", a=1)).then_inc(s_wo, 16)
            act.dma_start(gam[:], ln_gamma.partition_broadcast(P)).then_inc(s_gb, 16)
            act.dma_start(bet[:], ln_beta.partition_broadcast(P)).then_inc(s_gb, 16)
            act.dma_start(w_r[:], wr.rearrange("(c p) e -> p c e", p=P)).then_inc(s_wr, 16)
            act.dma_start(b_e[:], be).then_inc(s_be, 16)
            act.wait_ge(s_wqkv, 48)
            act.copy(w_qkv_s[0][:], w_qkv[:]).then_inc(s_wqkv_hi, 1)
            act.wait_ge(s_wctxT_ps, 1)
            act.copy(w_ctxT[:], bank[5][0:DC, 0:DC]).then_inc(s_wctxT, 1)
            act.wait_ge(s_cst, 16)
            act.wait_ge(s_wx, 32)
            act.wait_ge(s_const, 3)

            def body(i, front, back, rest):
                j = i - 1

                def transposed(n, b, banks, dst):
                    for t in range(TILES):
                        act.wait_ge(s_nT_ps[n], TILES * b + t + 1)
                        act.copy(dst[:, :, t * P:(t + 1) * P],
                                 banks[t][:, 0:D].rearrange("p (c n) -> p c n", c=KC)).then_inc(s_nT[n], 1)

                def values_queries_keys(t):
                    act.wait_ge(s_qkv_ps, TILES * i + t + 1)
                    act.copy(qk[:, t, :], bank[t][:]).then_inc(s_qk, 1)
                    vp = vpad[:, t].rearrange("p (k a) n -> p k (a n)", a=2)
                    for a in range(2):
                        o = nc.scalar.copy(vp[:, :, a * 48:a * 48 + DH],
                                           bank[2 + t][:, 0:D].rearrange("p (k a n) -> p k a n", a=2, n=DH)[:, :, a, :])
                    o.then_inc(s_v, 1)

                def softmax_exp(t):
                    act.wait_ge(s_nm, TILES * j + t + 1)
                    act.activation(ez[:, t], zb[:, t], ACT.Exp, bias=nmax[:, t:t + 1],
                                   accum_out=esum[:, t:t + 1]).then_inc(s_ez, 1)

                def head_queries(t):
                    act.wait_ge(s_qkT_ps, TILES * i + t + 1)
                    act.copy(kT[:, t], bank[t][:, D:].rearrange("p (g n) -> p g n", g=GROUPS))
                    for k in range(4):
                        o = act.activation(qx[:, t, :, k, :], bank[t][:, 0:D].rearrange("p (g n) -> p g n", g=GROUPS),
                                           ACT.Copy, scale=cst[:, C_PAR + k:C_PAR + k + 1])
                    o.then_inc(s_qkT, 1)

                def attention_out(t):
                    act.wait_ge(s_at_ps, TILES * i + t + 1)
                    src = bank[t][:, 0:D].rearrange("p (g n) -> p g n", g=GROUPS)
                    act.activation(sqT[:, t], src, ACT.Square)
                    act.copy(attT[:, t], src).then_inc(s_at, 1)

                if back:
                    transposed(1, j, bank[4:6], pT)
                if front:
                    transposed(0, i, bank[0:2], h1T[0])
                if back:
                    for t in range(TILES):
                        act.wait_ge(s_pk_ps, TILES * j + t + 1)
                        act.activation(pkvT[:, t * P:(t + 1) * P], bank[2 + t][0:DC, 0:P], ACT.Copy,
                                       scale=SIM_SCALE).then_inc(s_pk, 1)
                if front:
                    act.wait_ge(s_c_ps, 3 * i + 1)
                    act.copy(ctxT[:], bank[5][0:DC, 0:T]).then_inc(s_c, 1)
                    act.wait_ge(s_x, 16 * (i + 1))
                    if back:
                        act.wait_ge(s_x1, TILES * i)
                    act.copy(xres[:], xin[:]).then_inc(s_xres, 1)
                if back:
                    act.wait_ge(s_sb, i)
                    for t in range(TILES):
                        act.activation(z[:, t], bank[4][:, t * T:(t + 1) * T], ACT.Identity, bias=sim_b[:, t:t + 1],
                                       scale=rs[3][:, t:t + 1]).then_inc(s_z, 1)
                if front:
                    values_queries_keys(0)
                    act.wait_ge(s_c_ps, 3 * i + 2)
                    act.activation(kvT[:], bank[5][0:DC, 0:T], ACT.Identity, bias=b_ctx[:]).then_inc(s_c, 1)
                for t in range(TILES if back else 0):
                    softmax_exp(t)
                if front:
                    values_queries_keys(1)
                    act.wait_ge(s_c_ps, 3 * i + 3)
                    act.copy(kv[:], bank[5][:, 0:TILES * DC].rearrange("p (t d) -> p t d", t=TILES)).then_inc(s_c, 1)
                    for t in range(TILES):
                        head_queries(t)
                if front and not back:
                    act.wait_ge(s_wr, 16)
                    act.copy(w_r_s[0][:], w_r[:]).then_inc(s_hi, 1)
                    for c in range(KC):
                        act.wait_ge(s_we[c], 16)
                        act.copy(w_e_s[0][:, c], w_e[:, c]).then_inc(s_hi, 1)
                if back:
                    transposed(2, j, ebank, h3T[0])
                if front:
                    attention_out(0)
                if back:
                    act.wait_ge(s_gd, i)
                    act.activation(gexp[:], gdiff[:], ACT.Exp).then_inc(s_ge, 1)
                if front:
                    attention_out(1)
                if back:
                    act.wait_ge(s_gT_ps, i)
                    act.copy(gateT[:], ebank[1][0:E, 0:T]).then_inc(s_gT, 1)

            passes(act, body)

        @block.vector
        def _(dve):
            vf, vb = Count(FRONT_STEPS), Count(BACK_STEPS)

            def ln_stats(n, src, ready):
                for t in range(TILES):
                    nc.vector.bn_stats(stats[n][:, t, :], src(t))
                dve.drain()
                for t in range(TILES):
                    nc.vector.bn_aggr(mv[n][:, t, :], stats[n][:, t, :])
                dve.drain()
                nc.vector.tensor_scalar(ve[n][:], mv[n][:, :, 1], SIM_EPS if n == 3 else LN_EPS, None,
                                        ALU.add).then_inc(ready, 1)

            def ln_apply(n, src, b):
                dve.wait_ge(s_rstd[n], b + 1)
                for t in range(TILES):
                    nc.vector.tensor_scalar(norm[n][:, t, :], src[:, t, :], mv[n][:, t, 0:1], rs[n][:, t:t + 1],
                                            ALU.subtract, ALU.mult).then_inc(s_norm[n], 1)

            def low_parts(n, b, banks, dst):
                for t in range(TILES):
                    dve.wait_ge(s_nT[n], TILES * b + t + 1)
                    cols = slice(t * P, (t + 1) * P)
                    nc.vector.tensor_tensor(dst[1][:, :, cols], banks[t][:, 0:D].rearrange("p (c n) -> p c n", c=KC),
                                            dst[0][:, :, cols].bitcast(F32), ALU.subtract).then_inc(s_nT_lo[n], 1)

            def add_experts(b, u):
                t, q = divmod(u, E // 2)
                dve.wait_ge(s_ex, UNITS * b + u + 1)
                for k in range(2):
                    e = 2 * q + k
                    last = e == E - 1
                    if last and not (isinstance(b, int) and b == 0):
                        dve.wait_ge(s_st0 if t == 0 else s_st1, 16 * b)
                    nc.vector.scalar_tensor_tensor(
                        out=outb[:, t, :] if last else acc[:, t, :], in0=ebank[q % 2][:, k * D:(k + 1) * D],
                        scalar=gate[:, t, e:e + 1], in1=acc[:, t, :], op0=ALU.mult,
                        op1=ALU.add).then_inc(s_exd, 1)
                    if not last:
                        dve.wait_ge(s_exd, E * TILES * b + 2 * u + k + 1)

            def body(i, front, back, rest):
                j = i - 1
                vf.begin(i)
                vb.begin(j)

                def rotate(t):
                    dve.wait_ge(s_qk, TILES * i + t + 1)
                    rows = qk[:, t, :].rearrange("p (h r) -> p h r", r=DH // 2)[:, :, 0:ROT]
                    cos = cst[:, C_COS + t * ROT:C_COS + (t + 1) * ROT].unsqueeze(1).to_broadcast([P, 4 * H, ROT])
                    ra = rot_a[:, t].rearrange("p h a r -> p (h a) r")
                    rb = rot_b[:, t].rearrange("p h a r -> p (h a) r")
                    nc.vector.tensor_tensor(ra, rows, cos, ALU.mult).then_inc(v_front, vf.tick())
                    dve.wait_ge(v_front, vf.now())
                    dve.wait_ge(s_rb, 2 * (TILES * i + t + 1))
                    nc.vector.tensor_tensor(rows, ra, rb, ALU.add).then_inc(s_rot, 1)

                def softmax_input(t):
                    dve.wait_ge(s_z, TILES * j + t + 1)
                    nc.vector.tensor_tensor(zg[:, t], z[:, t], gam[:], ALU.mult)
                    dve.drain()
                    nc.vector.tensor_tensor_reduce(out=zb[:, t], in0=zg[:, t], in1=bet[:], scale=1.0,
                                                   scalar=-3.0e38, op0=ALU.add, op1=ALU.max,
                                                   accum_out=zmax[:, t:t + 1]).then_inc(v_back, vb.tick())
                    dve.wait_ge(v_back, vb.now())
                    nc.vector.tensor_scalar(nmax[:, t:t + 1], zmax[:, t:t + 1], -1.0, None,
                                            ALU.mult).then_inc(s_nm, 1)

                def residual2(t):
                    dve.wait_ge(s_ez, TILES * j + t + 1)
                    nc.vector.reciprocal(rsum[:, t:t + 1], esum[:, t:t + 1]).then_inc(v_back, vb.tick())
                    dve.wait_ge(v_back, vb.now())
                    nc.vector.scalar_tensor_tensor(out=x2[:, t, :], in0=ez[:, t], scalar=rsum[:, t:t + 1],
                                                   in1=x1[:, t, :], op0=ALU.mult, op1=ALU.add).then_inc(s_x2, 1)

                def decay_scores(t):
                    for n in range(QUADS):
                        dve.wait_ge(s_sc_ps, QUADS * (TILES * i + t) + n + 1)
                        nc.vector.tensor_tensor(probs[:, t, 4 * n:4 * n + 4, :],
                                                bank[2 + n][:].rearrange("p (h n) -> p h n", h=4),
                                                dec[:, 4 * n:4 * n + 4, :], ALU.mult).then_inc(s_sc, 1)

                def route():
                    dve.wait_ge(s_lg, i)
                    nc.vector.tensor_copy(lg[:], ebank[0][:, 0:TILES * E].rearrange("p (t e) -> p t e", e=E))
                    dve.drain()
                    for t in range(TILES):
                        nc.vector.max(top[:, t, :], lg[:, t, :]).then_inc(v_back, vb.tick())
                    dve.wait_ge(v_back, vb.now())
                    nc.vector.tensor_tensor(gdiff[:], top[:, :, 1], top[:, :, 0], ALU.subtract).then_inc(s_gd, 1)
                    for t in range(TILES):
                        nc.vector.max_index(idx[:, t, :], top[:, t, :], lg[:, t, :]).then_inc(v_back, vb.tick())
                    dve.wait_ge(v_back, vb.now())
                    nc.vector.tensor_copy(idxf[:], idx[:, :, 0:TOP]).then_inc(v_back, vb.tick())
                    dve.wait_ge(v_back, vb.now())
                    iota = cst[:, C_IOTA:C_IOTA + E].unsqueeze(1).to_broadcast([P, TILES, E])
                    for k in range(TOP):
                        nc.vector.tensor_tensor(onehot[:, k], iota, idxf[:, :, k:k + 1].to_broadcast([P, TILES, E]),
                                                ALU.is_equal)
                    dve.wait_ge(s_ge, i)
                    nc.vector.tensor_scalar(gden[:], gexp[:], 1.0, None, ALU.add).then_inc(v_back, vb.tick())
                    dve.wait_ge(v_back, vb.now())
                    nc.vector.reciprocal(gw[:, 0, :], gden[:]).then_inc(v_back, vb.tick())
                    dve.wait_ge(v_back, vb.now())
                    nc.vector.tensor_tensor(gw[:, 1, :], gexp[:], gw[:, 0, :], ALU.mult).then_inc(v_back, vb.tick())
                    dve.wait_ge(v_back, vb.now())
                    for k in range(TOP):
                        nc.vector.tensor_tensor(gpart[:, k], onehot[:, k],
                                                gw[:, k, :].unsqueeze(2).to_broadcast([P, TILES, E]),
                                                ALU.mult).then_inc(v_back, vb.tick())
                    dve.wait_ge(v_back, vb.now())
                    nc.vector.tensor_tensor(gate[:], gpart[:, 0], gpart[:, 1], ALU.add).then_inc(s_gate, 1)

                def late(u):
                    if rest:
                        add_experts(i - 2, u)

                def soon(u):
                    if back:
                        add_experts(j, u)

                if front:
                    dve.wait_ge(s_x, 16 * (i + 1))
                    ln_stats(0, lambda t: xin[:, t, :], s_var[0])
                late(3)
                if front:
                    ln_apply(0, xin, i)
                if front and not back:
                    dve.wait_ge(s_wqkv_hi, 1)
                    nc.vector.tensor_tensor(w_qkv_s[1][:], w_qkv[:], w_qkv_s[0][:].bitcast(F32),
                                            ALU.subtract).then_inc(s_wqkv_lo, 1)
                    dve.wait_ge(s_cst, 16)
                late(4)
                late(5)
                if front:
                    low_parts(0, i, bank[0:2], h1T)
                if back:
                    dve.wait_ge(s_sim, i)
                    ln_stats(3, lambda t: bank[4][:, t * T:(t + 1) * T], s_sv)
                late(6)
                if back:
                    dve.wait_ge(s_sr, i)
                    nc.vector.scalar_tensor_tensor(out=sim_b[:], in0=mv[3][:, :, 0], scalar=-1.0, in1=rs[3][:],
                                                   op0=ALU.mult, op1=ALU.mult).then_inc(s_sb, 1)
                if front and not back:
                    dve.wait_ge(s_wo, 16 * (1 + KC))
                    for c in range(KC):
                        nc.vector.tensor_scalar(w_o[:, c, :], w_o[:, c, :], rms_col[:, c:c + 1], None,
                                                ALU.mult).then_inc(s_wo_scaled, 1)
                    dve.wait_ge(s_gb, 32)
                if back:
                    softmax_input(0)
                    softmax_input(1)
                if front:
                    rotate(0)
                if back:
                    residual2(0)
                    residual2(1)
                if front:
                    rotate(1)
                if back:
                    dve.wait_ge(s_x2, TILES * i)
                    ln_stats(2, lambda t: x2[:, t, :], s_var[2])
                late(7)
                if back:
                    ln_apply(2, x2, j)
                if front:
                    if not back:
                        dve.wait_ge(s_dec, 16)
                    decay_scores(0)
                    dve.wait_ge(s_qkT, TILES * i + 2)
                    if back:
                        dve.wait_ge(s_at_ps, TILES * i)
                    nc.vector.tensor_tensor(qd[:], bank[1][:, 0:D].rearrange("p (g n) -> p g n", g=GROUPS),
                                            cst[:, C_QDEC:C_QDEC + D].rearrange("p (g n) -> p g n", g=GROUPS),
                                            ALU.mult).then_inc(s_qd, 1)
                if back:
                    low_parts(2, j, ebank, h3T)
                if front:
                    dve.wait_ge(s_st_ps, i + 1)
                    nc.vector.tensor_tensor(state[:], bank[0][:, 0:D].rearrange("p (g n) -> p g n", g=GROUPS),
                                            cst[:, C_BLOCK:C_BLOCK + P].unsqueeze(1).to_broadcast([P, GROUPS, P]),
                                            ALU.mult).then_inc(s_st, 1)
                if front and not back:
                    dve.wait_ge(s_hi, 1)
                    nc.vector.tensor_tensor(w_r_s[1][:], w_r[:], w_r_s[0][:].bitcast(F32), ALU.subtract).then_inc(s_lo, 1)
                if front:
                    decay_scores(1)
                if back:
                    route()
                if front:
                    for t in range(TILES):
                        dve.wait_ge(s_ss, TILES * i + t + 1)
                        nc.vector.tensor_scalar(rms_ve[:, t:t + 1], bank[4 + t][:, 0:1], 1.0 / D, RMS_EPS,
                                                ALU.mult, ALU.add).then_inc(s_rms_var, 1)
                if back:
                    dve.wait_ge(s_gb_ps, i)
                    nc.vector.tensor_tensor(acc[:], x2[:], ebank[0][:].rearrange("p (t n) -> p t n", t=TILES),
                                            ALU.add).then_inc(s_acc, 1)
                    dve.wait_ge(s_acc, i)
                if front:
                    dve.wait_ge(s_rms_rstd, i + 1)
                    dve.wait_ge(s_xres, i + 1)
                    for t in range(TILES):
                        dve.wait_ge(s_y, TILES * i + t + 1)
                        nc.vector.scalar_tensor_tensor(out=x1[:, t, :], in0=bank[2 + t][:, 0:D],
                                                       scalar=rms_rs[:, t:t + 1], in1=xres[:, t, :],
                                                       op0=ALU.mult, op1=ALU.add).then_inc(s_x1, 1)
                soon(0)
                if front:
                    dve.wait_ge(s_x1, TILES * i + 2)
                    ln_stats(1, lambda t: x1[:, t, :], s_var[1])
                soon(1)
                soon(2)
                if front:
                    ln_apply(1, x1, i)
                if not front and not back:
                    return
                assert (not front or vf.n == vf.each) and (not back or vb.n == vb.each), (vf.n, vb.n)

            passes(dve, body)

        @block.tensor
        def _(pe):
            pe.wait_ge(s_cst, 16)
            pe.wait_ge(s_wx, 32)
            pe.transpose(bank[5][0:DC, 0:DC], w_ctx[:], ident[0:DC, 0:DC]).then_inc(s_wctxT_ps, 1)
            pe.wait_ge(s_wctxT, 1)

            def split_product(dst, a, b, a_cols, b_cols):
                parts = [(0, 0), (1, 0), (0, 1)]
                for n, (ka, kb) in enumerate(parts):
                    for c in range(KC):
                        mm = pe.matmul(dst, a[ka][:, c, a_cols], b[kb][:, c, b_cols],
                                       start=(n == 0 and c == 0), stop=(n == 2 and c == KC - 1))
                return mm

            def transposes(n, b, banks):
                for t in range(TILES):
                    pe.wait_ge(s_norm[n], TILES * b + t + 1)
                    for c in range(KC):
                        mm = pe.transpose(banks[t][:, c * P:(c + 1) * P], norm[n][:, t, c * P:(c + 1) * P], ident)
                    mm.then_inc(s_nT_ps[n], 1)

            def body(i, front, back, rest):
                j = i - 1
                first = isinstance(i, int) and i == 0

                def expert_unit(there, b, u):
                    if not there:
                        return
                    t, q = divmod(u, E // 2)
                    if u == 0:
                        pe.wait_ge(s_acc, b + 1)
                    elif u >= 2:
                        pe.wait_ge(s_exd, 2 * (UNITS * b + u - 1))
                    split_product(ebank[q % 2][:], h3T, w_e_s, slice(t * P, (t + 1) * P),
                                  slice(2 * q * D, 2 * (q + 1) * D)).then_inc(s_ex, 1)

                def qkv(t):
                    pe.wait_ge(s_nT_lo[0], TILES * i + t + 1)
                    cols = slice(t * P, (t + 1) * P)
                    split_product(bank[t][:], h1T, w_qkv_s, cols, slice(0, 2 * D))
                    pe.wait_ge(s_c, 3 * i + 1 + t)
                    split_product(bank[2 + t][:, 0:D], h1T, w_qkv_s, cols, slice(2 * D, 3 * D)).then_inc(s_qkv_ps, 1)

                def scores(t):
                    pe.wait_ge(s_qkT, TILES * i + t + 1)
                    for g in range(GROUPS):
                        for half in range(2):
                            n = 2 * g + half
                            if t > 0:
                                pe.wait_ge(s_sc, QUADS * (TILES * i + t - 1) + n + 1)
                            rows = slice(64 * half, 64 * half + 64)
                            pe.matmul(bank[2 + n][:], kT[rows, t, g, :], qx[rows, t, g, :, :],
                                      start=True, stop=True).then_inc(s_sc_ps, 1)

                def state_product():
                    pe.wait_ge(s_kd, i + 1)
                    for g in range(GROUPS):
                        vg = vpad[:, 0].rearrange("p (k a) n -> p k (a n)", a=2)[:, g * PAIRS:(g + 1) * PAIRS]
                        vg = vg.rearrange("p k (u n) -> p k u n", n=DH)[:, :, 0:4:3, :]
                        mm = pe.matmul(bank[0][:, g * P:(g + 1) * P], kd[:, g * P:(g + 1) * P], vg,
                                       start=True, stop=True)
                    mm.then_inc(s_st_ps, 1)

                def attend(t):
                    if t == 0:
                        pe.wait_ge(s_st, i + 1)
                    else:
                        pe.wait_ge(s_qd, i + 1)
                    for g in range(GROUPS):
                        for par in range(2):
                            for q in range(PAIRS):
                                h = g * 8 + q * 2 + par
                                if h % 4 == 0:
                                    pe.wait_ge(s_sc, QUADS * (TILES * i + t) + h // 4 + 1)
                                mm = pe.matmul(bank[t][32 * q:32 * q + 32, g * P:(g + 1) * P], vpad[:, t, h, :],
                                               probs[:, t, h, :],
                                               start=(par == 0), stop=(par == 1 and t == 0))
                        if t == 1:
                            for q in range(PAIRS):
                                mm = pe.matmul(bank[t][32 * q:32 * q + 32, g * P:(g + 1) * P],
                                               state[:, g, 32 * q:32 * q + 32], qd[:, g, :], start=False, stop=True)
                    mm.then_inc(s_at_ps, 1)

                def project(t):
                    pe.wait_ge(s_at, TILES * i + t + 1)
                    for g in range(GROUPS):
                        mm = pe.matmul(bank[4 + t][:, 0:1], sqT[:, t, g, :], onescol[:],
                                       start=(g == 0), stop=(g == GROUPS - 1))
                    mm.then_inc(s_ss, 1)
                    for g in range(GROUPS):
                        mm = pe.matmul(bank[2 + t][:, 0:D], attT[:, t, g, :], w_o[:, g, :],
                                       start=(g == 0), stop=(g == GROUPS - 1))
                    mm.then_inc(s_y, 1)

                def late(u):
                    expert_unit(rest, i - 2, u)

                def soon(u):
                    expert_unit(back, j, u)

                late(3)
                late(4)
                if back:
                    transposes(1, j, bank[4:6])
                late(5)
                if front:
                    pe.wait_ge(s_ctx, 16 * (i + 1))
                    transposes(0, i, bank[0:2])
                if back:
                    pe.wait_ge(s_c, 3 * i)
                    for t in range(TILES):
                        pe.wait_ge(s_nT[1], TILES * j + t + 1)
                        for c in range(TILES):
                            mm = pe.matmul(bank[2 + t][0:DC, 0:P], kv[:, c, :], pT[:, c, t * P:(t + 1) * P],
                                           start=(c == 0), stop=(c == TILES - 1))
                        mm.then_inc(s_pk_ps, 1)
                if front:
                    for t in range(TILES):
                        mm = pe.transpose(bank[5][0:DC, t * P:(t + 1) * P], cin[:, t, :], ident)
                    mm.then_inc(s_c_ps, 1)
                if back:
                    for t in range(TILES):
                        pe.wait_ge(s_pk, TILES * j + t + 1)
                        mm = pe.matmul(bank[4][:, t * T:(t + 1) * T], pkvT[:, t * P:(t + 1) * P], kvT[:], start=True, stop=True)
                    mm.then_inc(s_sim, 1)
                late(6)
                if front:
                    if first:
                        pe.wait_ge(s_wqkv_lo, 1)
                    qkv(0)
                    pe.matmul(bank[5][0:DC, 0:T], w_ctxT[:], ctxT[:], start=True, stop=True).then_inc(s_c_ps, 1)
                    qkv(1)
                    for t in range(TILES):
                        mm = pe.transpose(bank[5][:, t * DC:(t + 1) * DC], kvT[:, t * P:(t + 1) * P], ident[0:DC, 0:DC])
                    mm.then_inc(s_c_ps, 1)
                    for t in range(TILES):
                        pe.wait_ge(s_rot, TILES * i + t + 1)
                        for b in range(2 * GROUPS):
                            mm = pe.transpose(bank[t][:, b * P:(b + 1) * P], qk[:, t, b * P:(b + 1) * P], ident)
                        mm.then_inc(s_qkT_ps, 1)
                        if t == 0:
                            late(7)
                else:
                    late(7)
                if front:
                    pe.wait_ge(s_c, 3 * i + 3)
                    scores(0)
                if back:
                    if rest:
                        pe.wait_ge(s_exd, 2 * UNITS * j)
                    transposes(2, j, ebank)
                if front:
                    state_product()
                if front:
                    scores(1)
                if back:
                    pe.wait_ge(s_lo, 1 + KC)
                    for t in range(TILES):
                        pe.wait_ge(s_nT_lo[2], TILES * j + t + 1)
                        mm = split_product(ebank[0][:, t * E:(t + 1) * E], h3T, w_r_s, slice(t * P, (t + 1) * P), slice(0, E))
                    mm.then_inc(s_lg, 1)
                if front:
                    attend(0)
                    attend(1)
                    pe.wait_ge(s_wo_scaled, KC)
                    project(0)
                if back:
                    pe.wait_ge(s_be, 16)
                    pe.wait_ge(s_gate, i)
                    for t in range(TILES):
                        mm = pe.transpose(ebank[1][0:E, t * P:(t + 1) * P], gate[:, t, :], ident)
                    mm.then_inc(s_gT_ps, 1)
                if front:
                    project(1)
                if back:
                    pe.wait_ge(s_gT, i)
                    for t in range(TILES):
                        mm = pe.matmul(ebank[0][:, t * D:(t + 1) * D], gateT[:, t * P:(t + 1) * P], b_e[:],
                                       start=True, stop=True)
                    mm.then_inc(s_gb_ps, 1)
                soon(0)
                soon(1)
                soon(2)

            passes(pe, body)


_INS = ["x", "ctx_512", "L0_attn_Wq", "L0_attn_Wk", "L0_attn_Wv", "L0_attn_Wo", "L0_attn_rms_w",
        "L0_xattn_W_k", "L0_xattn_b_k", "L0_xattn_ln_gamma", "L0_xattn_ln_beta",
        "L0_ffn_Wr", "L0_ffn_We", "L0_ffn_be"]


def kernel(**inputs):
    import concourse.bacc as _bacc
    from concourse.bass_utils import run_bass_kernel_spmd as _run

    nc = _bacc.Bacc("TRN2", target_bir_lowering=False, num_devices=1)
    arrays, args = {}, []
    small, decay = shape_constants()
    named = [(name, inputs[name]) for name in _INS] + [("consts", small), ("decay", decay)]
    for name, value in named:
        a = np.ascontiguousarray(value)
        arrays[f"in_{name}"] = a
        args.append(nc.dram_tensor(f"in_{name}", a.shape, mybir.dt.from_np(a.dtype), kind="ExternalInput").ap())
    args.append(nc.dram_tensor("out_0", (B, T, D), F32, kind="ExternalOutput").ap())
    decoder_layer(nc, *args)
    r = _run(nc, [arrays], core_ids=[0])
    return r.results[0]["out_0"]
```

```python
from contextlib import ExitStack

import numpy as np

import concourse.bass as bass
from concourse import mybir

F32 = mybir.dt.float32
F32R = mybir.dt.float32r
U32 = mybir.dt.uint32
ALU = mybir.AluOpType
ACT = mybir.ActivationFunctionType
AX_X = mybir.AxisListType.X

P = 128
B, T, D = 4, 256, 256
TILES = T // P
KC = D // P
H, DH = 16, 16
GROUPS = H * DH // P
PAIRS = 4
QUADS = H // 4
ROT = DH // 4
DC = 64
E, TOP = 8, 2
UNITS = TILES * E // 2
EARLY = 6
LN_EPS, RMS_EPS, SIM_EPS = 1e-5, 1e-5, 1e-6
SIM_SCALE = T ** -0.5
FRONT_STEPS, BACK_STEPS = 2, 16

C_IDENT = 0
C_COS = C_IDENT + P
C_SIN = C_COS + TILES * ROT
C_KDEC = C_SIN + TILES * 2 * ROT
C_QDEC = C_KDEC + H
C_PICK = C_QDEC + GROUPS * P
C_BLOCK = C_PICK + 4
C_IOTA = C_BLOCK + P
C_ALL = C_IOTA + E


def shape_constants():
    f = np.float32
    start = 2.0 ** (-2.0 ** (-(np.log2(H) - 3)))
    slopes = np.array([start * start ** i for i in range(H)], f)
    r = np.exp(-slopes.astype(np.float64))
    pos = np.arange(P)
    c = np.zeros((P, C_ALL), f)
    c[:, C_IDENT:C_IDENT + P] = np.eye(P, dtype=f)
    freq = (f(1.0 / 1024.0) ** np.linspace(0.0, 1.0, ROT, dtype=f)).astype(f)
    theta = (np.arange(T, dtype=f)[:, None] * freq[None, :]).astype(f).astype(np.float64)
    cos = np.cos(theta).reshape(TILES, P, ROT).transpose(1, 0, 2)
    sin = np.sin(theta).reshape(TILES, P, ROT).transpose(1, 0, 2)
    c[:, C_COS:C_SIN] = cos.reshape(P, -1)
    c[:, C_SIN:C_KDEC] = np.stack([sin, -sin], axis=2).reshape(P, -1)
    c[:, C_KDEC:C_QDEC] = r[None, :] ** (P - 1.0 - pos[:, None])
    head_of_row = np.arange(P) // DH
    for g in range(GROUPS):
        c[:, C_QDEC + g * P:C_QDEC + (g + 1) * P] = r[g * 8 + head_of_row][:, None] ** (pos[None, :] + 1.0)
    c[:, C_PICK:C_BLOCK] = (head_of_row[:, None] % 4) == np.arange(4)[None, :]
    c[:, C_BLOCK:C_IOTA] = head_of_row[:, None] == head_of_row[None, :]
    c[:, C_IOTA:] = np.arange(E)[None, :]
    diff = pos[None, :] - pos[:, None]
    decay = np.where(diff[:, None, :] >= 0, r[None, :, None] ** np.maximum(diff, 0)[:, None, :], 0.0)
    return c, decay.astype(f).reshape(P, H * P)


class Count:

    def __init__(self, each):
        self.each, self.n, self.i = each, 0, 0

    def begin(self, i):
        self.i, self.n = i, 0

    def tick(self):
        self.n += 1
        return 1

    def now(self):
        return self.i * self.each + self.n


def decoder_layer(nc, x, ctx, wq, wk, wv, wo, rms_w, w_k, b_k, ln_gamma, ln_beta, wr, we, be,
                  consts, decay, out):
    with ExitStack() as stack:
        def sb(name, shape, dt=F32):
            return stack.enter_context(nc.sbuf_tensor(name, shape, dt))

        def sem(name):
            return stack.enter_context(nc.semaphore(name))

        cst = sb("cst", [P, C_ALL])
        dec = sb("dec", [P, H, P])
        w_qkv = sb("w_qkv", [P, KC, 3 * D])
        w_qkv_s = [sb(f"w_qkv_{n}", [P, KC, 3 * D], F32R) for n in ("hi", "lo")]
        w_o = sb("w_o", [P, KC, D])
        rms_col = sb("rms_col", [P, KC])
        w_ctx = sb("w_ctx", [DC, DC])
        w_ctxT = sb("w_ctxT", [DC, TILES * DC])
        b_ctx = sb("b_ctx", [TILES * DC, 1])
        gam = sb("gam", [P, T])
        bet = sb("bet", [P, T])
        w_r = sb("w_r", [P, KC, E])
        w_r_s = sb("w_r_hi_lo", [P, KC, 2, E], F32R)
        w_e = sb("w_e", [P, KC, E * D])
        w_e_s = [sb(f"w_e_{n}", [P, KC, E * D], F32R) for n in ("hi", "lo")]
        b_e = sb("b_e", [P, D])
        b_e_s = sb("b_e_parts", [P, D], F32R)
        nhalf = sb("nhalf", [P, 2])
        act_warm = sb("act_warm", [P, 2])
        onescol = sb("onescol", [P, 1])
        ident = cst[:, C_IDENT:C_IDENT + P]
        xin = sb("xin", [P, TILES, D])
        xres = sb("xres", [P, TILES, D])
        cin = sb("cin", [P, TILES, DC])
        ctxT = sb("ctxT", [DC, T])
        kvT = sb("kvT", [TILES * DC, T])
        kv = sb("kv", [P, TILES, DC])
        stats = [sb(f"stats{n}", [P, TILES, 6]) for n in range(4)]
        mv = [sb(f"mv{n}", [P, TILES, 2]) for n in range(4)]
        ve = [sb(f"ve{n}", [P, TILES]) for n in range(4)]
        rs = [sb(f"rs{n}", [P, TILES]) for n in range(4)]
        norm = [sb(f"norm{n}", [P, TILES, D]) for n in range(3)]
        h1T = [sb(f"h1T_{n}", [P, KC, T], F32R) for n in ("hi", "lo")]
        qk = sb("qk", [P, TILES, 2 * D])
        rot_a = sb("rot_a", [P, TILES, 2 * H, 2, ROT])
        rot_b = sb("rot_b", [P, TILES, 2 * H, 2, ROT])
        vpad = sb("vpad", [P, TILES, H, 2 * DH])
        qx = sb("qx", [P, TILES, GROUPS, 4, P])
        kT = sb("kT", [P, TILES, GROUPS, P])
        kd = sb("kd", [P, D])
        qd = sb("qd", [P, GROUPS, P])
        state = sb("state", [P, GROUPS, P])
        probs = sb("probs", [P, TILES, H, P])
        attT = sb("attT", [P, TILES, GROUPS, P])
        sqT = sb("sqT", [P, TILES, GROUPS, P])
        rms_ve = sb("rms_ve", [P, TILES])
        rms_rs = sb("rms_rs", [P, TILES])
        x1 = sb("x1", [P, TILES, D])
        pT = sb("pT", [P, KC, T])
        pkvT = sb("pkvT", [TILES * DC, P])
        sim_b = sb("sim_b", [P, TILES])
        z = sb("z", [P, TILES, T])
        zg = sb("zg", [P, TILES, T])
        zb = sb("zb", [P, TILES, T])
        zmax = sb("zmax", [P, TILES])
        nmax = sb("nmax", [P, TILES])
        ez = sb("ez", [P, TILES, T])
        esum = sb("esum", [P, TILES])
        rsum = sb("rsum", [P, TILES])
        x2 = sb("x2", [P, TILES, D])
        h3T = [sb(f"h3T_{n}", [P, KC, T], F32R) for n in ("hi", "lo")]
        lg = sb("lg", [P, TILES, E])
        top = sb("top", [P, TILES, 8])
        idx = sb("idx", [P, TILES, 8], U32)
        idxf = sb("idxf", [P, TILES, TOP])
        onehot = sb("onehot", [P, TOP, TILES, E])
        gdiff = sb("gdiff", [P, TILES])
        gexp = sb("gexp", [P, TILES])
        gden = sb("gden", [P, TILES])
        gw = sb("gw", [P, TOP, TILES])
        gpart = sb("gpart", [P, TOP, TILES, E])
        gate = sb("gate", [P, TILES, E])
        gate_s = sb("gate_parts", [P, TILES, P], F32R)
        gateT = sb("gateT", [P, T], F32R)
        biases = sb("biases", [P, TILES, D])
        acc = sb("acc", [P, TILES, D])
        outb = sb("outb", [P, TILES, D])

        bank = [stack.enter_context(nc.psum_tensor(f"bank{n}", [P, 512], F32)) for n in range(6)]
        ebank = [stack.enter_context(nc.psum_tensor(f"ebank{n}", [P, 512], F32)) for n in range(2)]

        def is_last(b):
            return isinstance(b, int) and b == B - 1

        def biases_after(b):
            return 8 if isinstance(b, int) and b >= B - 2 else 12

        def expert_bank(b, u):
            if isinstance(b, int) and b == B - 2 and u >= EARLY:
                return bank[5 if u == 6 else 0]
            return bank[u] if 2 <= u < (EARLY if is_last(b) else 4) else ebank[(u + 1) % 2]

        s_x, s_ctx = sem("x_loaded"), sem("ctx_loaded")
        s_cst, s_dec, s_wo, s_wx, s_bx, s_gb, s_wr, s_be = (
            sem(f"{n}_loaded") for n in ("consts", "decay", "wo", "wctx", "bctx", "gamma_beta", "wr", "be"))
        s_wqkv = [sem(f"{n}_loaded") for n in ("wq", "wk", "wv")]
        s_we = [sem(f"we{k}_loaded") for k in range(KC)]
        s_const = sem("pool_consts_ready")
        s_hi, s_lo = sem("weights_high_parts"), sem("weights_low_parts")
        s_be_hi, s_be_lo = sem("biases_high_parts"), sem("biases_low_part")
        s_wqkv_hi, s_wqkv_lo = sem("wqkv_high_parts"), sem("wqkv_low_parts")
        v_front, v_back = sem("vector_front_step"), sem("vector_back_step")
        s_wo_scaled = sem("wo_scaled")
        s_wctxT_ps, s_wctxT = sem("wctxT_in_psum"), sem("wctxT_ready")
        s_var = [sem(f"ln{n}_variance") for n in (1, 2, 3)]
        s_rstd = [sem(f"ln{n}_rstd") for n in (1, 2, 3)]
        s_norm = [sem(f"ln{n}_normalized") for n in (1, 2, 3)]
        s_nT_ps = [sem(f"ln{n}_transposed") for n in (1, 2, 3)]
        s_nT = [sem(f"ln{n}_T_on_sbuf") for n in (1, 2, 3)]
        s_nT_lo = [sem(f"ln{n}_T_low_part") for n in (1, 2, 3)]
        s_xres = sem("residual_copied")
        s_qkv_ps, s_qk, s_v = sem("qkv_in_psum"), sem("qk_on_sbuf"), sem("v_on_sbuf")
        s_rb, s_rot, s_kd = sem("rotary_cross_terms"), sem("rotated"), sem("k_decayed")
        s_qkT_ps, s_qkT, s_qd = sem("qkT_in_psum"), sem("qkT_on_sbuf"), sem("q_decayed")
        s_st_ps, s_st = sem("state_in_psum"), sem("state_masked")
        s_sc_ps, s_sc = sem("scores_in_psum"), sem("scores_decayed")
        s_at_ps, s_at = sem("attention_in_psum"), sem("attention_on_sbuf")
        s_ss, s_y = sem("square_sums"), sem("attention_projected")
        s_rms_var, s_rms_rstd, s_x1 = sem("rms_variance"), sem("rms_rstd"), sem("x1_ready")
        s_c_ps, s_c = sem("context_step_in_psum"), sem("context_step_on_sbuf")
        s_pk_ps, s_pk = sem("pkv_in_psum"), sem("pkv_on_sbuf")
        s_sim = sem("similarity_in_psum")
        s_sv, s_sr, s_sb = sem("sim_variance"), sem("sim_rstd"), sem("sim_shift")
        s_z, s_nm, s_ez, s_x2 = (sem("sim_normalized"), sem("sim_negmax"), sem("sim_exp"), sem("x2_ready"))
        s_gate_s = sem("gate_parts_ready")
        s_lg, s_lg_read, s_gd, s_ge, s_gate = sem("logits"), sem("logits_read"), sem("gate_difference"), sem("gate_exp"), sem("gates_ready")
        s_gT_ps, s_gT, s_gb_ps, s_gb_sb, s_acc = (sem("gatesT_in_psum"), sem("gatesT_on_sbuf"),
                                         sem("expert_bias_in_psum"), sem("expert_bias_on_sbuf"), sem("biases_added"))
        s_ex, s_exd = sem("expert_pair_in_psum"), sem("expert_products_added")
        s_st0, s_st1 = sem("tile0_stored"), sem("tile1_stored")

        block = stack.enter_context(nc.Block())

        def passes(eng, body):
            body(0, True, False, False)
            body(1, True, True, False)
            with eng.Fori(2, B) as i:
                body(i, True, True, True)
            body(B, False, True, True)
            body(B + 1, False, False, True)

        @block.sync
        def _(sp):
            def load_x(i):
                sp.dma_start(xin[:], x[i].rearrange("(t p) d -> p t d", p=P)).then_inc(s_x, 16)

            load_x(0)
            for n, w in enumerate((wq, wk, wv)):
                sp.dma_start(w_qkv[:, :, n * D:(n + 1) * D], w.rearrange("(c p) n -> p c n", p=P)).then_inc(s_wqkv[n], 16)
            for t in range(TILES):
                sp.dma_start(b_ctx[t * DC:(t + 1) * DC], b_k.rearrange("(p a) -> p a", a=1)).then_inc(s_bx, 16)
            sp.dma_start(dec[:], decay.rearrange("p (h n) -> p h n", h=H)).then_inc(s_dec, 16)
            sp.dma_start(w_o[:], wo.rearrange("(c p) n -> p c n", p=P)).then_inc(s_wo, 16)
            for c in range(KC):
                sp.dma_start(rms_col[:, c:c + 1], rms_w[c * P:(c + 1) * P].rearrange("(p a) -> p a", a=1)).then_inc(s_wo, 16)
            for c in range(KC):
                sp.dma_start(w_e[:, c].rearrange("p (e f) -> p e f", e=E),
                             we.rearrange("e (c p) f -> p c e f", p=P)[:, c]).then_inc(s_we[c], 16)
            sp.dma_start(gam[:], ln_gamma.partition_broadcast(P)).then_inc(s_gb, 16)
            sp.dma_start(bet[:], ln_beta.partition_broadcast(P)).then_inc(s_gb, 16)
            sp.dma_start(w_r[:], wr.rearrange("(c p) e -> p c e", p=P)).then_inc(s_wr, 16)
            sp.wait_ge(s_const, 5)
            for k in range(3):
                sp.dma_start(b_e[32 * k:32 * k + E], be).then_inc(s_be, 16)

            def body(i, front, back, experts):
                if front and back:
                    sp.wait_ge(s_norm[0], TILES * i)
                    sp.wait_ge(s_xres, i)
                    load_x(i)
                    sp.wait_ge(s_c_ps, 3 * (i - 1) + 1)
                    sp.dma_start(cin[:], ctx[i].rearrange("(t p) d -> p t d", p=P)).then_inc(s_ctx, 16)
                if experts:
                    b = i - 2
                    for t, done in ((0, s_st0), (1, s_st1)):
                        sp.wait_ge(s_exd, TILES * E * (b + 1) - 1 + t)
                        sp.dma_start(out[b].rearrange("(t p) d -> p t d", p=P)[:, t, :], outb[:, t, :]).then_inc(done, 16)

            passes(sp, body)
            sp.wait_ge(s_st0, 16 * B)
            sp.wait_ge(s_st1, 16 * B)

        @block.gpsimd
        def _(pool):
            nc.gpsimd.memset(nhalf[:], -0.5).then_inc(s_const, 1)
            nc.gpsimd.memset(onescol[:], 1.0).then_inc(s_const, 1)
            nc.gpsimd.memset(vpad[:], 0.0).then_inc(s_const, 1)
            nc.gpsimd.memset(b_e[:], 0.0).then_inc(s_const, 1)
            nc.gpsimd.memset(gate_s[:].bitcast(F32), 0.0).then_inc(s_const, 1)
            pool.wait_ge(s_const, 5)

            def rsqrt(dst, src, i, ready, done, each=1):
                pool.wait_ge(ready, each * (i + 1))
                nc.gpsimd.tensor_tensor(dst[:], src[:], nhalf[:], ALU.pow).then_inc(done, 1)

            def body(i, front, back, experts):
                if back:
                    rsqrt(rs[1], ve[1], i - 1, s_var[1], s_rstd[1])
                if front:
                    rsqrt(rs[0], ve[0], i, s_var[0], s_rstd[0])
                if experts:
                    pool.wait_ge(s_gb_sb, i - 1)
                    pool.wait_ge(s_exd, TILES * E * (i - 2) + biases_after(i - 2))
                    nc.gpsimd.tensor_tensor(acc[:], acc[:], biases[:], ALU.add).then_inc(s_acc, 1)
                if back:
                    rsqrt(rs[3], ve[3], i - 1, s_sv, s_sr)
                for t in range(TILES if front else 0):
                    pool.wait_ge(s_qk, TILES * i + t + 1)
                    v = qk[:, t, :].rearrange("p (h a r) -> p h a r", a=2, r=DH // 2)
                    for a in range(2):
                        at = C_SIN + (t * 2 + a) * ROT
                        sin = cst[:, at:at + ROT].unsqueeze(1).to_broadcast([P, 2 * H, ROT])
                        nc.gpsimd.tensor_tensor(rot_b[:, t, :, a, :], v[:, :, 1 - a, 0:ROT], sin,
                                                ALU.mult).then_inc(s_rb, 1)
                if front:
                    pool.wait_ge(s_rot, TILES * i + 1)
                    kdec = cst[:, C_KDEC:C_KDEC + H].unsqueeze(2).to_broadcast([P, H, DH])
                    nc.gpsimd.tensor_tensor(kd[:].rearrange("p (h d) -> p h d", h=H),
                                            qk[:, 0, D:].rearrange("p (h d) -> p h d", h=H), kdec,
                                            ALU.mult).then_inc(s_kd, 1)
                if back:
                    rsqrt(rs[2], ve[2], i - 1, s_var[2], s_rstd[2])
                if front and not back:
                    pool.wait_ge(s_hi, 2)
                    nc.gpsimd.tensor_tensor(w_e_s[1][:, 0], w_e[:, 0], w_e_s[0][:, 0].bitcast(F32),
                                            ALU.subtract).then_inc(s_lo, 1)
                if front:
                    rsqrt(rms_rs, rms_ve, i, s_rms_var, s_rms_rstd, TILES)

            passes(pool, body)

        @block.scalar
        def _(act):
            act.dma_start(cst[:], consts).then_inc(s_cst, 16)
            act.wait_ge(s_const, 1)
            act.activation(act_warm[:], nhalf[:], ACT.Exp)
            act.dma_start(cin[:], ctx[0].rearrange("(t p) d -> p t d", p=P)).then_inc(s_ctx, 16)
            act.dma_start(w_ctx[:], w_k).then_inc(s_wx, 16)
            act.wait_ge(s_cst, 16)
            act.wait_ge(s_const, 5)

            def body(i, front, back, experts):
                j = i - 1
                ln3_banks = ebank if front else bank[2:4]
                pkv_bank, sim_banks = (bank[2], bank[3:5]) if front else (bank[0], (bank[4], bank[1]))

                def high_weights(n):
                    act.wait_ge(s_wqkv[n], 16)
                    act.copy(w_qkv_s[0][:, :, n * D:(n + 1) * D], w_qkv[:, :, n * D:(n + 1) * D]).then_inc(s_wqkv_hi, 1)

                def transposed(n, b, banks, dst):
                    for t in range(TILES):
                        act.wait_ge(s_nT_ps[n], TILES * b + t + 1)
                        act.copy(dst[:, :, t * P:(t + 1) * P],
                                 banks[t][:, 0:D].rearrange("p (c n) -> p c n", c=KC)).then_inc(s_nT[n], 1)

                def queries_keys(t):
                    act.wait_ge(s_qkv_ps, TILES * i + t + 1)
                    act.copy(qk[:, t, :], bank[t][:]).then_inc(s_qk, 1)

                def values(t):
                    vp = vpad[:, t].rearrange("p (k a) n -> p k (a n)", a=2)
                    for a in range(2):
                        o = nc.scalar.copy(vp[:, :, a * 48:a * 48 + DH],
                                           bank[2 + t][:, 0:D].rearrange("p (k a n) -> p k a n", a=2, n=DH)[:, :, a, :])
                    o.then_inc(s_v, 1)

                def normalize_similarities(t):
                    act.activation(z[:, t], sim_banks[t][:, 0:T], ACT.Identity, bias=sim_b[:, t:t + 1],
                                   scale=rs[3][:, t:t + 1]).then_inc(s_z, 1)

                def softmax_exp(t):
                    act.wait_ge(s_nm, TILES * j + t + 1)
                    act.activation(ez[:, t], zb[:, t], ACT.Exp, bias=nmax[:, t:t + 1],
                                   accum_out=esum[:, t:t + 1]).then_inc(s_ez, 1)

                def head_queries(t):
                    act.wait_ge(s_qkT_ps, TILES * i + t + 1)
                    act.copy(kT[:, t], bank[t][:, D:].rearrange("p (g n) -> p g n", g=GROUPS))
                    for k in range(4):
                        o = act.activation(qx[:, t, :, k, :], bank[t][:, 0:D].rearrange("p (g n) -> p g n", g=GROUPS),
                                           ACT.Copy, scale=cst[:, C_PICK + k:C_PICK + k + 1])
                    o.then_inc(s_qkT, 1)

                def attention_out(t):
                    act.wait_ge(s_at_ps, TILES * i + t + 1)
                    src = bank[t][:, 0:D].rearrange("p (g n) -> p g n", g=GROUPS)
                    act.activation(sqT[:, t], src, ACT.Square)
                    act.copy(attT[:, t], src).then_inc(s_at, 1)

                if back:
                    transposed(1, j, bank[4:6], pT)
                if front and not back:
                    high_weights(0)
                if front:
                    transposed(0, i, bank[0:2], h1T[0])
                if front and not back:
                    high_weights(1)
                    high_weights(2)
                    act.wait_ge(s_wctxT_ps, 1)
                    for t in range(TILES):
                        act.copy(w_ctxT[:, t * DC:(t + 1) * DC], bank[4][0:DC, 0:DC]).then_inc(s_wctxT, 1)
                if back:
                    act.wait_ge(s_pk_ps, i)
                    act.activation(pkvT[:], pkv_bank[:, 0:P], ACT.Copy, scale=SIM_SCALE).then_inc(s_pk, 1)
                if front:
                    act.wait_ge(s_c_ps, 3 * i + 1)
                    act.copy(ctxT[:], bank[5][0:DC, 0:T]).then_inc(s_c, 1)
                    act.wait_ge(s_x, 16 * (i + 1))
                    if back:
                        act.wait_ge(s_x1, TILES * i)
                    act.copy(xres[:], xin[:]).then_inc(s_xres, 1)
                if back:
                    act.wait_ge(s_sb, i)
                    normalize_similarities(0)
                    normalize_similarities(1)
                if front:
                    queries_keys(0)
                    values(0)
                    act.wait_ge(s_c_ps, 3 * i + 2)
                    if not back:
                        act.wait_ge(s_bx, 32)
                    act.activation(kvT[:], bank[5][:, 0:T], ACT.Identity, bias=b_ctx[:]).then_inc(s_c, 1)
                if back:
                    softmax_exp(0)
                if front:
                    queries_keys(1)
                    head_queries(0)
                if back:
                    softmax_exp(1)
                if front:
                    values(1)
                    act.wait_ge(s_c_ps, 3 * i + 3)
                    act.copy(kv[:], bank[5][:, 0:TILES * DC].rearrange("p (t d) -> p t d", t=TILES)).then_inc(s_c, 1)
                    head_queries(1)
                if front and not back:
                    act.wait_ge(s_be, 48)
                    act.copy(b_e_s[:], b_e[:]).then_inc(s_be_hi, 1)
                    act.wait_ge(s_wr, 16)
                    act.copy(w_r_s[:, :, 0, :], w_r[:]).then_inc(s_hi, 1)
                    for c in range(KC):
                        act.wait_ge(s_we[c], 16)
                        act.copy(w_e_s[0][:, c], w_e[:, c]).then_inc(s_hi, 1)
                if back:
                    transposed(2, j, ln3_banks, h3T[0])
                if front:
                    attention_out(0)
                if back:
                    act.wait_ge(s_gd, i)
                    act.activation(gexp[:], gdiff[:], ACT.Exp).then_inc(s_ge, 1)
                if front:
                    attention_out(1)
                if back:
                    act.wait_ge(s_gT_ps, i)
                    act.copy(gateT[:], bank[0][:, 0:T]).then_inc(s_gT, 1)
                    act.wait_ge(s_gb_ps, i)
                    if experts:
                        act.wait_ge(s_acc, i - 1)
                    act.copy(biases[:], bank[1][:].rearrange("p (t n) -> p t n", t=TILES)).then_inc(s_gb_sb, 1)

            passes(act, body)

        @block.vector
        def _(dve):
            vf, vb = Count(FRONT_STEPS), Count(BACK_STEPS)

            def ln_stats(n, src, ready):
                for t in range(TILES):
                    nc.vector.bn_stats(stats[n][:, t, :], src(t))
                dve.drain()
                for t in range(TILES):
                    nc.vector.bn_aggr(mv[n][:, t, :], stats[n][:, t, :])
                dve.drain()
                nc.vector.tensor_scalar(ve[n][:], mv[n][:, :, 1], SIM_EPS if n == 3 else LN_EPS, None,
                                        ALU.add).then_inc(ready, 1)

            def ln_apply(n, src, b):
                dve.wait_ge(s_rstd[n], b + 1)
                for t in range(TILES):
                    nc.vector.tensor_scalar(norm[n][:, t, :], src[:, t, :], mv[n][:, t, 0:1], rs[n][:, t:t + 1],
                                            ALU.subtract, ALU.mult).then_inc(s_norm[n], 1)

            def low_parts(n, b, banks, dst):
                for t in range(TILES):
                    dve.wait_ge(s_nT[n], TILES * b + t + 1)
                    cols = slice(t * P, (t + 1) * P)
                    nc.vector.tensor_tensor(dst[1][:, :, cols], banks[t][:, 0:D].rearrange("p (c n) -> p c n", c=KC),
                                            dst[0][:, :, cols].bitcast(F32), ALU.subtract).then_inc(s_nT_lo[n], 1)

            def add_units(b, q):
                for n in range(4 * q, 4 * q + 4):
                    e, t = divmod(n, TILES)
                    u = TILES * q + t
                    dve.wait_ge(s_ex, UNITS * b + u + 1)
                    if n == 0:
                        dve.wait_ge(s_gate, b + 1)
                    if n == biases_after(b):
                        dve.wait_ge(s_acc, b + 1)
                    last = e == E - 1
                    if last and not (isinstance(b, int) and b == 0):
                        dve.wait_ge(s_st0 if t == 0 else s_st1, 16 * b)
                    if e:
                        dve.wait_ge(s_exd, TILES * E * b + n - 1)
                    nc.vector.scalar_tensor_tensor(
                        out=outb[:, t, :] if last else acc[:, t, :],
                        in0=expert_bank(b, u)[:, (e % 2) * D:(e % 2 + 1) * D],
                        scalar=gate[:, t, e:e + 1], in1=acc[:, t, :] if e else x2[:, t, :],
                        op0=ALU.mult, op1=ALU.add).then_inc(s_exd, 1)

            def body(i, front, back, experts):
                j = i - 1
                ln3_banks = ebank if front else bank[2:4]
                pkv_bank, sim_banks = (bank[2], bank[3:5]) if front else (bank[0], (bank[4], bank[1]))
                vf.begin(i)
                vb.begin(j)

                def low_weights(n):
                    dve.wait_ge(s_wqkv_hi, n + 1)
                    nc.vector.tensor_tensor(w_qkv_s[1][:, :, n * D:(n + 1) * D], w_qkv[:, :, n * D:(n + 1) * D],
                                            w_qkv_s[0][:, :, n * D:(n + 1) * D].bitcast(F32),
                                            ALU.subtract).then_inc(s_wqkv_lo, 1)

                def rotate(t):
                    dve.wait_ge(s_qk, TILES * i + t + 1)
                    rows = qk[:, t, :].rearrange("p (h r) -> p h r", r=DH // 2)[:, :, 0:ROT]
                    cos = cst[:, C_COS + t * ROT:C_COS + (t + 1) * ROT].unsqueeze(1).to_broadcast([P, 4 * H, ROT])
                    ra = rot_a[:, t].rearrange("p h a r -> p (h a) r")
                    rb = rot_b[:, t].rearrange("p h a r -> p (h a) r")
                    nc.vector.tensor_tensor(ra, rows, cos, ALU.mult).then_inc(v_front, vf.tick())
                    dve.wait_ge(v_front, vf.now())
                    dve.wait_ge(s_rb, 2 * (TILES * i + t + 1))
                    nc.vector.tensor_tensor(rows, ra, rb, ALU.add).then_inc(s_rot, 1)

                def softmax_input(t):
                    dve.wait_ge(s_z, TILES * j + t + 1)
                    nc.vector.tensor_tensor(zg[:, t], z[:, t], gam[:], ALU.mult)
                    dve.drain()
                    nc.vector.tensor_tensor_reduce(out=zb[:, t], in0=zg[:, t], in1=bet[:], scale=1.0,
                                                   scalar=-3.0e38, op0=ALU.add, op1=ALU.max,
                                                   accum_out=zmax[:, t:t + 1]).then_inc(v_back, vb.tick())
                    dve.wait_ge(v_back, vb.now())
                    nc.vector.tensor_scalar(nmax[:, t:t + 1], zmax[:, t:t + 1], -1.0, None,
                                            ALU.mult).then_inc(s_nm, 1)

                def residual2(t):
                    dve.wait_ge(s_ez, TILES * j + t + 1)
                    nc.vector.reciprocal(rsum[:, t:t + 1], esum[:, t:t + 1]).then_inc(v_back, vb.tick())
                    dve.wait_ge(v_back, vb.now())
                    nc.vector.scalar_tensor_tensor(out=x2[:, t, :], in0=ez[:, t], scalar=rsum[:, t:t + 1],
                                                   in1=x1[:, t, :], op0=ALU.mult, op1=ALU.add).then_inc(s_x2, 1)

                def decay_scores(t):
                    for n in range(QUADS):
                        dve.wait_ge(s_sc_ps, QUADS * (TILES * i + t) + n + 1)
                        nc.vector.tensor_tensor(probs[:, t, 4 * n:4 * n + 4, :],
                                                bank[2 + n][:].rearrange("p (h n) -> p h n", h=4),
                                                dec[:, 4 * n:4 * n + 4, :], ALU.mult).then_inc(s_sc, 1)

                def route():
                    dve.wait_ge(s_lg, i)
                    lgp = ln3_banks[0][:, 0:TILES * 2 * E].rearrange("p (t n e) -> p t e n", n=2, e=E)
                    nc.vector.tensor_reduce(lg[:], lgp, AX_X, ALU.add).then_inc(s_lg_read, 1)
                    dve.drain()
                    for t in range(TILES):
                        nc.vector.max(top[:, t, :], lg[:, t, :]).then_inc(v_back, vb.tick())
                    dve.wait_ge(v_back, vb.now())
                    nc.vector.tensor_tensor(gdiff[:], top[:, :, 1], top[:, :, 0], ALU.subtract).then_inc(s_gd, 1)
                    for t in range(TILES):
                        nc.vector.max_index(idx[:, t, :], top[:, t, :], lg[:, t, :]).then_inc(v_back, vb.tick())
                    dve.wait_ge(v_back, vb.now())
                    nc.vector.tensor_copy(idxf[:], idx[:, :, 0:TOP]).then_inc(v_back, vb.tick())
                    dve.wait_ge(v_back, vb.now())
                    iota = cst[:, C_IOTA:C_IOTA + E].unsqueeze(1).to_broadcast([P, TILES, E])
                    for k in range(TOP):
                        nc.vector.tensor_tensor(onehot[:, k], iota, idxf[:, :, k:k + 1].to_broadcast([P, TILES, E]),
                                                ALU.is_equal)
                    dve.wait_ge(s_ge, i)
                    nc.vector.tensor_scalar(gden[:], gexp[:], 1.0, None, ALU.add).then_inc(v_back, vb.tick())
                    dve.wait_ge(v_back, vb.now())
                    nc.vector.reciprocal(gw[:, 0, :], gden[:]).then_inc(v_back, vb.tick())
                    dve.wait_ge(v_back, vb.now())
                    nc.vector.tensor_tensor(gw[:, 1, :], gexp[:], gw[:, 0, :], ALU.mult).then_inc(v_back, vb.tick())
                    dve.wait_ge(v_back, vb.now())
                    for k in range(TOP):
                        nc.vector.tensor_tensor(gpart[:, k], onehot[:, k],
                                                gw[:, k, :].unsqueeze(2).to_broadcast([P, TILES, E]),
                                                ALU.mult).then_inc(v_back, vb.tick())
                    dve.wait_ge(v_back, vb.now())
                    nc.vector.tensor_tensor(gate[:], gpart[:, 0], gpart[:, 1], ALU.add).then_inc(s_gate, 1)
                    dve.wait_ge(s_gate, i)
                    nc.vector.tensor_copy(gate_s[:, :, 0:E], gate[:]).then_inc(v_back, vb.tick())
                    nc.vector.tensor_copy(gate_s[:, :, 64:64 + E], gate[:]).then_inc(v_back, vb.tick())
                    dve.wait_ge(v_back, vb.now())
                    nc.vector.tensor_tensor(gate_s[:, :, 32:32 + E], gate[:], gate_s[:, :, 0:E].bitcast(F32),
                                            ALU.subtract).then_inc(s_gate_s, 1)

                def late(steady=None, last=None):
                    q = steady if front else last
                    if experts and q is not None:
                        add_units(i - 2, q)

                if not front and not back:
                    for q in range(E // 2):
                        add_units(i - 2, q)
                    return
                if back:
                    dve.wait_ge(s_x1, TILES * i)
                    ln_stats(1, lambda t: x1[:, t, :], s_var[1])
                if front:
                    dve.wait_ge(s_x, 16 * (i + 1))
                    ln_stats(0, lambda t: xin[:, t, :], s_var[0])
                if back:
                    ln_apply(1, x1, j)
                late(steady=0, last=0)
                if front:
                    ln_apply(0, xin, i)
                late(steady=1)
                late(steady=2)
                if front and not back:
                    low_weights(0)
                if front:
                    low_parts(0, i, bank[0:2], h1T)
                if front and not back:
                    low_weights(1)
                    low_weights(2)
                    dve.wait_ge(s_cst, 16)
                late(last=1)
                if back:
                    dve.wait_ge(s_sim, i)
                    ln_stats(3, lambda t: sim_banks[t][:, 0:T], s_sv)
                    dve.wait_ge(s_sr, i)
                    nc.vector.scalar_tensor_tensor(out=sim_b[:], in0=mv[3][:, :, 0], scalar=-1.0, in1=rs[3][:],
                                                   op0=ALU.mult, op1=ALU.mult).then_inc(s_sb, 1)
                late(last=2)
                if back:
                    softmax_input(0)
                if front:
                    rotate(0)
                if back:
                    softmax_input(1)
                    residual2(0)
                if front:
                    rotate(1)
                if back:
                    residual2(1)
                    dve.wait_ge(s_x2, TILES * i)
                    ln_stats(2, lambda t: x2[:, t, :], s_var[2])
                late(steady=3)
                if back:
                    ln_apply(2, x2, j)
                late(last=3)
                if front:
                    if not back:
                        dve.wait_ge(s_dec, 16)
                    decay_scores(0)
                    dve.wait_ge(s_qkT, TILES * i + 2)
                    if back:
                        dve.wait_ge(s_at_ps, TILES * i)
                    nc.vector.tensor_tensor(qd[:], bank[1][:, 0:D].rearrange("p (g n) -> p g n", g=GROUPS),
                                            cst[:, C_QDEC:C_QDEC + D].rearrange("p (g n) -> p g n", g=GROUPS),
                                            ALU.mult).then_inc(s_qd, 1)
                if back:
                    low_parts(2, j, ln3_banks, h3T)
                if front:
                    dve.wait_ge(s_st_ps, i + 1)
                    nc.vector.tensor_tensor(state[:], bank[0][:, 0:D].rearrange("p (g n) -> p g n", g=GROUPS),
                                            cst[:, C_BLOCK:C_BLOCK + P].unsqueeze(1).to_broadcast([P, GROUPS, P]),
                                            ALU.mult).then_inc(s_st, 1)
                if front and not back:
                    dve.wait_ge(s_be_hi, 1)
                    nc.vector.tensor_tensor(b_e_s[64:96], b_e[64:96], b_e_s[64:96].bitcast(F32), ALU.subtract).then_inc(s_be_lo, 1)
                    dve.wait_ge(s_hi, 1)
                    nc.vector.tensor_tensor(w_r_s[:, :, 1, :], w_r[:], w_r_s[:, :, 0, :].bitcast(F32), ALU.subtract).then_inc(s_lo, 1)
                if front:
                    decay_scores(1)
                if back:
                    route()
                if front and not back:
                    dve.wait_ge(s_hi, 3)
                    nc.vector.tensor_tensor(w_e_s[1][:, 1], w_e[:, 1], w_e_s[0][:, 1].bitcast(F32),
                                            ALU.subtract).then_inc(s_lo, 1)
                    dve.wait_ge(s_wo, 16 * (1 + KC))
                    for c in range(KC):
                        nc.vector.tensor_scalar(w_o[:, c, :], w_o[:, c, :], rms_col[:, c:c + 1], None,
                                                ALU.mult).then_inc(s_wo_scaled, 1)
                    dve.wait_ge(s_gb, 32)
                if front:
                    for t in range(TILES):
                        dve.wait_ge(s_ss, TILES * i + t + 1)
                        nc.vector.tensor_scalar(rms_ve[:, t:t + 1], bank[4 + t][:, 0:1], 1.0 / D, RMS_EPS,
                                                ALU.mult, ALU.add).then_inc(s_rms_var, 1)
                    dve.wait_ge(s_rms_rstd, i + 1)
                    dve.wait_ge(s_xres, i + 1)
                    for t in range(TILES):
                        dve.wait_ge(s_y, TILES * i + t + 1)
                        nc.vector.scalar_tensor_tensor(out=x1[:, t, :], in0=bank[2 + t][:, 0:D],
                                                       scalar=rms_rs[:, t:t + 1], in1=xres[:, t, :],
                                                       op0=ALU.mult, op1=ALU.add).then_inc(s_x1, 1)
                assert (not front or vf.n == vf.each) and (not back or vb.n == vb.each), (vf.n, vb.n)

            passes(dve, body)

        @block.tensor
        def _(pe):
            pe.wait_ge(s_cst, 16)

            def split_product(dst, a, b, a_cols, b_cols):
                parts = [(0, 0), (1, 0), (0, 1)]
                for n, (ka, kb) in enumerate(parts):
                    for c in range(KC):
                        mm = pe.matmul(dst, a[ka][:, c, a_cols], b[kb][:, c, b_cols],
                                       start=(n == 0 and c == 0), stop=(n == 2 and c == KC - 1))
                return mm

            def keep_clock(n, dst):
                for _ in range(n):
                    pe.matmul(dst[:], ident, cst[:, 0:512], start=True, stop=True)

            def transposes(n, b, banks):
                for t in range(TILES):
                    pe.wait_ge(s_norm[n], TILES * b + t + 1)
                    for c in range(KC):
                        mm = pe.transpose(banks[t][:, c * P:(c + 1) * P], norm[n][:, t, c * P:(c + 1) * P], ident)
                    mm.then_inc(s_nT_ps[n], 1)

            def body(i, front, back, experts):
                j = i - 1
                ln3_banks = ebank if front else bank[2:4]
                pkv_bank, sim_banks = (bank[2], bank[3:5]) if front else (bank[0], (bank[4], bank[1]))
                first = isinstance(i, int) and i == 0

                def expert_unit(b, u):
                    q, t = divmod(u, TILES)
                    if is_last(b):
                        if u < 2:
                            pe.wait_ge(s_exd, TILES * E * (b - 1) + 8 + 3 + t)
                        elif u == 2:
                            pe.wait_ge(s_lg_read, b + 1)
                        elif u >= EARLY:
                            pe.wait_ge(s_exd, TILES * E * b + 3 + t)
                    elif u == 1:
                        pe.wait_ge(s_lg_read, b + 1)
                    elif u in (2, 3):
                        pe.wait_ge(s_x1, TILES * (b + 1) + t + 1)
                    elif isinstance(b, int) and b == B - 2 and u >= EARLY:
                        pass
                    elif u >= 4:
                        pe.wait_ge(s_exd, TILES * E * b + (0 if u < 6 else 8) + 3 + t)
                    split_product(expert_bank(b, u)[:], h3T, w_e_s, slice(t * P, (t + 1) * P),
                                  slice(2 * q * D, 2 * (q + 1) * D)).then_inc(s_ex, 1)

                def qkv(t):
                    pe.wait_ge(s_nT_lo[0], TILES * i + t + 1)
                    cols = slice(t * P, (t + 1) * P)
                    split_product(bank[t][:], h1T, w_qkv_s, cols, slice(0, 2 * D))
                    if first and t == 0:
                        pe.wait_ge(s_wqkv_lo, 3)
                    if t == 0:
                        pe.wait_ge(s_c, 3 * i + 1)
                    elif back:
                        pe.wait_ge(s_z, TILES * i)
                    split_product(bank[2 + t][:, 0:D], h1T, w_qkv_s, cols, slice(2 * D, 3 * D)).then_inc(s_qkv_ps, 1)

                def scores(t):
                    pe.wait_ge(s_v, TILES * (i + 1))
                    pe.wait_ge(s_qkT, TILES * i + t + 1)
                    for g in range(GROUPS):
                        for half in range(2):
                            n = 2 * g + half
                            if t > 0:
                                pe.wait_ge(s_sc, QUADS * (TILES * i + t - 1) + n + 1)
                            rows = slice(64 * half, 64 * half + 64)
                            pe.matmul(bank[2 + n][:], kT[rows, t, g, :], qx[rows, t, g, :, :],
                                      start=True, stop=True).then_inc(s_sc_ps, 1)

                def state_product():
                    pe.wait_ge(s_kd, i + 1)
                    for g in range(GROUPS):
                        vg = vpad[:, 0].rearrange("p (k a) n -> p k (a n)", a=2)[:, g * PAIRS:(g + 1) * PAIRS]
                        vg = vg.rearrange("p k (u n) -> p k u n", n=DH)[:, :, 0:4:3, :]
                        mm = pe.matmul(bank[0][:, g * P:(g + 1) * P], kd[:, g * P:(g + 1) * P], vg,
                                       start=True, stop=True)
                    mm.then_inc(s_st_ps, 1)

                def attend(t):
                    if t == 0:
                        pe.wait_ge(s_st, i + 1)
                    else:
                        pe.wait_ge(s_qd, i + 1)
                    for g in range(GROUPS):
                        for par in range(2):
                            for q in range(PAIRS):
                                h = g * 8 + q * 2 + par
                                if h % 4 == 0:
                                    pe.wait_ge(s_sc, QUADS * (TILES * i + t) + h // 4 + 1)
                                mm = pe.matmul(bank[t][32 * q:32 * q + 32, g * P:(g + 1) * P], vpad[:, t, h, :],
                                               probs[:, t, h, :],
                                               start=(par == 0), stop=(par == 1 and t == 0))
                        if t == 1:
                            for q in range(PAIRS):
                                mm = pe.matmul(bank[t][32 * q:32 * q + 32, g * P:(g + 1) * P],
                                               state[:, g, 32 * q:32 * q + 32], qd[:, g, :], start=False, stop=True)
                    mm.then_inc(s_at_ps, 1)

                def project(t):
                    pe.wait_ge(s_at, TILES * i + t + 1)
                    for g in range(GROUPS):
                        mm = pe.matmul(bank[4 + t][:, 0:1], sqT[:, t, g, :], onescol[:],
                                       start=(g == 0), stop=(g == GROUPS - 1))
                    mm.then_inc(s_ss, 1)
                    for g in range(GROUPS):
                        mm = pe.matmul(bank[2 + t][:, 0:D], attT[:, t, g, :], w_o[:, g, :],
                                       start=(g == 0), stop=(g == GROUPS - 1))
                    mm.then_inc(s_y, 1)

                def late(steady=(), last=()):
                    for u in (steady if front else last) if experts else ():
                        if back or u >= EARLY:
                            expert_unit(i - 2, u)

                if front and back and not experts:
                    keep_clock(3, ebank[0])
                late(steady=(0, 1, 2, 3, 4), last=(0, 1))
                if back:
                    transposes(1, j, bank[4:6])
                late(steady=(5,), last=(2,))
                if front:
                    if experts:
                        pe.wait_ge(s_gb_sb, i - 1)
                    pe.wait_ge(s_ctx, 16 * (i + 1))
                    transposes(0, i, bank[0:2])
                if back:
                    if experts and front:
                        pe.wait_ge(s_exd, TILES * E * (i - 2) + 7)
                    pe.wait_ge(s_c, 3 * i)
                    pe.wait_ge(s_nT[1], TILES * i)
                    for c in range(TILES):
                        for t in range(TILES):
                            mm = pe.matmul(pkv_bank[t * DC:(t + 1) * DC, 0:P], kv[:, c, :], pT[:, c, t * P:(t + 1) * P],
                                           start=(c == 0), stop=(c == TILES - 1))
                    mm.then_inc(s_pk_ps, 1)
                late(last=(3,))
                if front:
                    for t in range(TILES):
                        mm = pe.transpose(bank[5][0:DC, t * P:(t + 1) * P], cin[:, t, :], ident)
                    mm.then_inc(s_c_ps, 1)
                if first:
                    pe.wait_ge(s_wx, 16)
                    pe.transpose(bank[4][0:DC, 0:DC], w_ctx[:], ident[0:DC, 0:DC]).then_inc(s_wctxT_ps, 1)
                if back:
                    if experts and front:
                        pe.wait_ge(s_exd, TILES * E * (i - 2) + 8)
                    pe.wait_ge(s_pk, i)
                    for t in range(TILES):
                        half = slice(t * DC, (t + 1) * DC)
                        mm = pe.matmul(sim_banks[t][:, 0:T], pkvT[half, :], kvT[half, :], start=True, stop=True)
                    mm.then_inc(s_sim, 1)
                if first:
                    keep_clock(1, ebank[0])
                late(steady=(6,), last=(4, 5, 6, 7))
                if back and not front:
                    pe.wait_ge(s_exd, TILES * E * (i - 2) + 8)
                    keep_clock(6, bank[2])
                if front:
                    if first:
                        pe.wait_ge(s_wqkv_lo, 2)
                    qkv(0)
                    if first:
                        pe.wait_ge(s_wctxT, TILES)
                    pe.matmul(bank[5][:, 0:T], w_ctxT[:], ctxT[:], start=True, stop=True).then_inc(s_c_ps, 1)
                    qkv(1)
                    for t in range(TILES):
                        if t == 0:
                            pe.wait_ge(s_c, 3 * i + 2)
                        pe.wait_ge(s_rot, TILES * i + t + 1)
                        for b in range(2 * GROUPS):
                            mm = pe.transpose(bank[t][:, b * P:(b + 1) * P], qk[:, t, b * P:(b + 1) * P], ident)
                        mm.then_inc(s_qkT_ps, 1)
                        if t == 0:
                            for c in range(TILES):
                                mm = pe.transpose(bank[5][:, c * DC:(c + 1) * DC], kvT[0:DC, c * P:(c + 1) * P], ident[0:DC, 0:DC])
                            mm.then_inc(s_c_ps, 1)
                            late(steady=(7,))
                            if not experts:
                                keep_clock(2, ebank[0])
                    pe.wait_ge(s_c, 3 * i + 3)
                    scores(0)
                if back:
                    if front and experts:
                        pe.wait_ge(s_exd, TILES * E * j)
                    transposes(2, j, ln3_banks)
                    if not front:
                        pe.wait_ge(s_z, TILES * i)
                        keep_clock(1, bank[1])
                if front:
                    state_product()
                    scores(1)
                if back:
                    pe.wait_ge(s_lo, 1 + KC)
                    for t in range(TILES):
                        pe.wait_ge(s_nT_lo[2], TILES * j + t + 1)
                        for n in range(2):
                            for c in range(KC):
                                w = w_r_s[:, c] if n == 0 else w_r_s[:, c, 0]
                                dst = ln3_banks[0][:, t * 2 * E:(t * 2 + 2 - n) * E]
                                mm = pe.matmul(dst, h3T[n][:, c, t * P:(t + 1) * P], w,
                                               start=(n == 0 and c == 0), stop=(n == 1 and c == KC - 1))
                    mm.then_inc(s_lg, 1)
                if front:
                    attend(0)
                    attend(1)
                    pe.wait_ge(s_wo_scaled, KC)
                    project(0)
                elif back:
                    for u in range(3):
                        expert_unit(j, u)
                if back:
                    pe.wait_ge(s_be_lo, 1)
                    if not front:
                        pe.wait_ge(s_exd, TILES * E * j)
                    pe.wait_ge(s_gate_s, i)
                    for t in range(TILES):
                        mm = pe.transpose(bank[0][:, t * P:(t + 1) * P], gate_s[:, t, :].bitcast(F32), ident)
                    mm.then_inc(s_gT_ps, 1)
                if front:
                    project(1)
                elif back:
                    expert_unit(j, 3)
                if back:
                    pe.wait_ge(s_gT, i)
                    for t in range(TILES):
                        mm = pe.matmul(bank[1][:, t * D:(t + 1) * D], gateT[:, t * P:(t + 1) * P], b_e_s[:],
                                       start=True, stop=True)
                    mm.then_inc(s_gb_ps, 1)
                if back and not front:
                    for u in range(4, EARLY):
                        expert_unit(j, u)

            passes(pe, body)


_INS = ["x", "ctx_512", "L0_attn_Wq", "L0_attn_Wk", "L0_attn_Wv", "L0_attn_Wo", "L0_attn_rms_w",
        "L0_xattn_W_k", "L0_xattn_b_k", "L0_xattn_ln_gamma", "L0_xattn_ln_beta",
        "L0_ffn_Wr", "L0_ffn_We", "L0_ffn_be"]


def kernel(**inputs):
    import concourse.bacc as _bacc
    from concourse.bass_utils import run_bass_kernel_spmd as _run

    nc = _bacc.Bacc("TRN2", target_bir_lowering=False, num_devices=1)
    arrays, args = {}, []
    small, decay = shape_constants()
    named = [(name, inputs[name]) for name in _INS] + [("consts", small), ("decay", decay)]
    for name, value in named:
        a = np.ascontiguousarray(value)
        arrays[f"in_{name}"] = a
        args.append(nc.dram_tensor(f"in_{name}", a.shape, mybir.dt.from_np(a.dtype), kind="ExternalInput").ap())
    args.append(nc.dram_tensor("out_0", (B, T, D), F32, kind="ExternalOutput").ap())
    decoder_layer(nc, *args)
    r = _run(nc, [arrays], core_ids=[0])
    return r.results[0]["out_0"]
```
